# Optimizing a Trainium2 kernel written in Bass

```python
import numpy as np
import jax
import jax.numpy as jnp

def _softmax(x, axis=-1):
    return jax.nn.softmax(x, axis=axis)

def _gelu(x):
    return jax.nn.gelu(x, approximate=True)

def _silu(x):
    return jax.nn.silu(x)

def _sigmoid(x):
    return jax.nn.sigmoid(x)

def _layernorm(x, axis=-1, eps=1e-05):
    m = jnp.mean(x, axis=axis, keepdims=True)
    v = jnp.var(x, axis=axis, keepdims=True)
    return (x - m) / jnp.sqrt(v + eps)

def _scatter_add(tgt, idx, src, axis=0):
    return tgt.at[idx].add(src)

def _segment_sum(src, seg, n):
    return jax.ops.segment_sum(src, seg, n)
kernel_name = 'mk_cond_seq_d2_seqx_r8_fc58ea'

def setup_inputs(seed: int=0):
    np.random.seed(seed)
    _w = jnp.asarray

    def _rec_inputs():
        import jax
        import jax.numpy as jnp
        _rk = jax.random.key(seed)
        x = -0.0002928 + 1 * jax.random.normal(jax.random.fold_in(_rk, 1), (2, 512, 128), jnp.float32)
        _lenS = 512 - jax.random.randint(jax.random.fold_in(_rk, 7), (2,), 0, max(1, 512 // 4) + 1, jnp.int32)
        _lenS2 = 512 - jax.random.randint(jax.random.fold_in(_rk, 8), (2,), 0, max(1, 512 // 4) + 1, jnp.int32)
        itok_B_6_14 = jax.random.randint(jax.random.fold_in(_rk, 11), (2,), 6, 15, jnp.int32)
        condB_theta = jax.random.uniform(jax.random.fold_in(_rk, 12), (2,), jnp.float32, 0.0, 0.983423)
        condB_phi = jax.random.uniform(jax.random.fold_in(_rk, 13), (2,), jnp.float32, 0.0, 0.961312)
        return (x, itok_B_6_14, condB_theta, condB_phi)
    x, itok_B_6_14, condB_theta, condB_phi = _rec_inputs()

    def _L0_cond_setup():
        import jax, jax.numpy as jnp
        import numpy as np
        D = 128
        E = 8
        FF = 512
        TOPK = 2
        S = 32
        SE = 64
        SH = 128
        B, T = (2, 256)

        def _forward(x, subject_ids, ln_g, ln_b, subj_emb, hyp_w1, hyp_b1, hyp_w2, hyp_b2, sty_w1, sty_b1, sty_w2, sty_b2, router_w, exp_w1, exp_b1, exp_w2, exp_b2):
            mu = x.mean(-1, keepdims=True)
            var = x.var(-1, keepdims=True)
            h = (x - mu) * jax.lax.rsqrt(var + 1e-05) * ln_g + ln_b
            m_t = h.mean(1, keepdims=True)
            v_t = h.var(1, keepdims=True)
            h_norm = (h - m_t) * jax.lax.rsqrt(v_t + 1e-08)
            se = subj_emb[subject_ids]
            hyp = jax.nn.relu(se @ hyp_w1 + hyp_b1) @ hyp_w2 + hyp_b2
            sty = jax.nn.relu(hyp @ sty_w1 + sty_b1) @ sty_w2 + sty_b2
            gamma, beta = jnp.split(sty, 2, axis=-1)
            gamma = jax.nn.softplus(gamma) + 1e-08
            h = h_norm * gamma[:, None, :] + beta[:, None, :]
            h_flat = h.reshape(-1, D)
            probs = jax.nn.softmax(h_flat @ router_w, axis=-1)
            gates, idx = jax.lax.top_k(probs, TOPK)
            gates = gates / gates.sum(-1, keepdims=True)
            N = h_flat.shape[0]
            combine = jnp.zeros((N, E), h_flat.dtype).at[jnp.arange(N)[:, None], idx].add(gates)
            hid = jax.nn.relu(jnp.einsum('nd,edf->nef', h_flat, exp_w1) + exp_b1)
            eout = jnp.einsum('nef,efd->ned', hid, exp_w2) + exp_b2
            y = jnp.einsum('ned,ne->nd', eout, combine)
            return x + y.reshape(x.shape)
        key = jax.random.key(seed)
        ks = jax.random.split(key, 16)
        n = lambda k, sh, s=0.02: jax.random.normal(k, sh, dtype=jnp.float32) * s
        return {'x': jax.random.normal(ks[0], (B, T, D), dtype=jnp.float32), 'subject_ids': jax.random.randint(ks[1], (B,), 0, S), 'ln_g': jnp.ones((D,), jnp.float32), 'ln_b': jnp.zeros((D,), jnp.float32), 'subj_emb': n(ks[2], (S, SE)), 'hyp_w1': n(ks[3], (SE, SH), 1.0 / np.sqrt(SE)), 'hyp_b1': jnp.zeros((SH,), jnp.float32), 'hyp_w2': n(ks[4], (SH, SH), 1.0 / np.sqrt(SH)), 'hyp_b2': jnp.zeros((SH,), jnp.float32), 'sty_w1': n(ks[5], (SH, SH // 2), 1.0 / np.sqrt(SH)), 'sty_b1': jnp.zeros((SH // 2,), jnp.float32), 'sty_w2': n(ks[6], (SH // 2, 2 * D), 1.0 / np.sqrt(SH // 2)), 'sty_b2': jnp.zeros((2 * D,), jnp.float32), 'router_w': n(ks[7], (D, E), 1.0 / np.sqrt(D)), 'exp_w1': n(ks[8], (E, D, FF), 1.0 / np.sqrt(D)), 'exp_b1': jnp.zeros((E, FF), jnp.float32), 'exp_w2': n(ks[9], (E, FF, D), 1.0 / np.sqrt(FF)), 'exp_b2': jnp.zeros((E, D), jnp.float32)}
    _L0_cond_all = _L0_cond_setup()
    _L0_cond_in = {k: v for k, v in _L0_cond_all.items() if k in ('ln_g', 'ln_b', 'subj_emb', 'hyp_w1', 'hyp_b1', 'hyp_w2', 'hyp_b2', 'sty_w1', 'sty_b1', 'sty_w2', 'sty_b2', 'router_w', 'exp_w1', 'exp_b1', 'exp_w2', 'exp_b2')}
    del _L0_cond_all

    def _L1_cond_setup():
        import jax, jax.numpy as jnp
        import numpy as np
        key = jax.random.key(seed)
        k1, k2, k3 = jax.random.split(key, 3)
        B, N, D = (16, 512, 128)
        embeddings = jax.random.normal(k1, (B, N, D), dtype=jnp.float32)
        theta = jax.random.uniform(k2, (B,), dtype=jnp.float32)
        phi = jax.random.uniform(k3, (B,), dtype=jnp.float32)
        return {'embeddings': embeddings, 'theta': theta, 'phi': phi}
    _L1_cond_all = _L1_cond_setup()
    _L1_cond_in = {k: v for k, v in _L1_cond_all.items() if k in ()}
    del _L1_cond_all
    return {'x': x, 'itok_B_6_14': itok_B_6_14, 'condB_theta': condB_theta, 'condB_phi': condB_phi, 'L0_cond_ln_g': _L0_cond_in['ln_g'], 'L0_cond_ln_b': _L0_cond_in['ln_b'], 'L0_cond_subj_emb': _L0_cond_in['subj_emb'], 'L0_cond_hyp_w1': _L0_cond_in['hyp_w1'], 'L0_cond_hyp_b1': _L0_cond_in['hyp_b1'], 'L0_cond_hyp_w2': _L0_cond_in['hyp_w2'], 'L0_cond_hyp_b2': _L0_cond_in['hyp_b2'], 'L0_cond_sty_w1': _L0_cond_in['sty_w1'], 'L0_cond_sty_b1': _L0_cond_in['sty_b1'], 'L0_cond_sty_w2': _L0_cond_in['sty_w2'], 'L0_cond_sty_b2': _L0_cond_in['sty_b2'], 'L0_cond_router_w': _L0_cond_in['router_w'], 'L0_cond_exp_w1': _L0_cond_in['exp_w1'], 'L0_cond_exp_b1': _L0_cond_in['exp_b1'], 'L0_cond_exp_w2': _L0_cond_in['exp_w2'], 'L0_cond_exp_b2': _L0_cond_in['exp_b2']}

def reference(x, itok_B_6_14, condB_theta, condB_phi, L0_cond_ln_g, L0_cond_ln_b, L0_cond_subj_emb, L0_cond_hyp_w1, L0_cond_hyp_b1, L0_cond_hyp_w2, L0_cond_hyp_b2, L0_cond_sty_w1, L0_cond_sty_b1, L0_cond_sty_w2, L0_cond_sty_b2, L0_cond_router_w, L0_cond_exp_w1, L0_cond_exp_b1, L0_cond_exp_w2, L0_cond_exp_b2):
    import jax
    import jax.numpy as jnp

    def _L0_cond_ref(x, subject_ids, ln_g, ln_b, subj_emb, hyp_w1, hyp_b1, hyp_w2, hyp_b2, sty_w1, sty_b1, sty_w2, sty_b2, router_w, exp_w1, exp_b1, exp_w2, exp_b2):
        import jax, jax.numpy as jnp
        import numpy as np
        D = 128
        E = 8
        FF = 512
        TOPK = 2
        S = 32
        SE = 64
        SH = 128
        B, T = (2, 256)

        def _forward(x, subject_ids, ln_g, ln_b, subj_emb, hyp_w1, hyp_b1, hyp_w2, hyp_b2, sty_w1, sty_b1, sty_w2, sty_b2, router_w, exp_w1, exp_b1, exp_w2, exp_b2):
            mu = x.mean(-1, keepdims=True)
            var = x.var(-1, keepdims=True)
            h = (x - mu) * jax.lax.rsqrt(var + 1e-05) * ln_g + ln_b
            m_t = h.mean(1, keepdims=True)
            v_t = h.var(1, keepdims=True)
            h_norm = (h - m_t) * jax.lax.rsqrt(v_t + 1e-08)
            se = subj_emb[subject_ids]
            hyp = jax.nn.relu(se @ hyp_w1 + hyp_b1) @ hyp_w2 + hyp_b2
            sty = jax.nn.relu(hyp @ sty_w1 + sty_b1) @ sty_w2 + sty_b2
            gamma, beta = jnp.split(sty, 2, axis=-1)
            gamma = jax.nn.softplus(gamma) + 1e-08
            h = h_norm * gamma[:, None, :] + beta[:, None, :]
            h_flat = h.reshape(-1, D)
            probs = jax.nn.softmax(h_flat @ router_w, axis=-1)
            gates, idx = jax.lax.top_k(probs, TOPK)
            gates = gates / gates.sum(-1, keepdims=True)
            N = h_flat.shape[0]
            combine = jnp.zeros((N, E), h_flat.dtype).at[jnp.arange(N)[:, None], idx].add(gates)
            hid = jax.nn.relu(jnp.einsum('nd,edf->nef', h_flat, exp_w1) + exp_b1)
            eout = jnp.einsum('nef,efd->ned', hid, exp_w2) + exp_b2
            y = jnp.einsum('ned,ne->nd', eout, combine)
            return x + y.reshape(x.shape)
        return _forward(x, subject_ids, ln_g, ln_b, subj_emb, hyp_w1, hyp_b1, hyp_w2, hyp_b2, sty_w1, sty_b1, sty_w2, sty_b2, router_w, exp_w1, exp_b1, exp_w2, exp_b2)

    def _L1_cond_ref(embeddings, theta, phi):
        import jax, jax.numpy as jnp
        import numpy as np
        B, N, D = embeddings.shape
        e = embeddings.reshape(B, N, D // 4, 4)
        ct = jnp.cos(theta)[:, None, None]
        st = jnp.sin(theta)[:, None, None]
        cp = jnp.cos(phi)[:, None, None]
        sp = jnp.sin(phi)[:, None, None]
        x0, x1, x2, x3 = (e[..., 0], e[..., 1], e[..., 2], e[..., 3])
        out = jnp.stack([x0 * ct + x1 * st, -x0 * st + x1 * ct, x2 * cp + x3 * sp, -x2 * sp + x3 * cp], axis=-1)
        return out.reshape(B, N, D)
    x = _L0_cond_ref(x, itok_B_6_14, L0_cond_ln_g, L0_cond_ln_b, L0_cond_subj_emb, L0_cond_hyp_w1, L0_cond_hyp_b1, L0_cond_hyp_w2, L0_cond_hyp_b2, L0_cond_sty_w1, L0_cond_sty_b1, L0_cond_sty_w2, L0_cond_sty_b2, L0_cond_router_w, L0_cond_exp_w1, L0_cond_exp_b1, L0_cond_exp_w2, L0_cond_exp_b2)
    x = _L1_cond_ref(x, condB_theta, condB_phi)
    return x

_drawn_inputs = setup_inputs


def setup_inputs(seed=0):
    import zlib

    import numpy as np

    out = dict(_drawn_inputs(seed))
    spreads = {'L0_cond_ln_g': (1.0, 0.2),
     'L0_cond_ln_b': (0.0, 0.1),
     'L0_cond_hyp_b1': (0.0, 0.1),
     'L0_cond_hyp_b2': (0.0, 0.1),
     'L0_cond_sty_b1': (0.0, 0.1),
     'L0_cond_sty_b2': (0.0, 0.1),
     'L0_cond_exp_b1': (0.0, 0.1),
     'L0_cond_exp_b2': (0.0, 0.1)}
    factors = {}
    for name, (base, spread) in spreads.items():
        noise = np.random.default_rng([zlib.crc32(name.encode()), seed]).standard_normal(out[name].shape)
        drawn = base * np.exp(spread * noise) if base else spread * noise
        out[name] = jnp.asarray(drawn.astype(out[name].dtype))
    for name, factor in factors.items():
        out[name] = (out[name] * factor).astype(out[name].dtype)
    return out
```

```python
import math
from contextlib import ExitStack

import concourse.bass as bass
from concourse import mybir

ALU = mybir.AluOpType
ACT = mybir.ActivationFunctionType
AX_X = mybir.AxisListType.X
F32 = mybir.dt.float32
F32R = mybir.dt.float32r
I32 = mybir.dt.int32

P = 128
B = 2
T = 512
TT = T // P
E = 8
FF = 512
FC = FF // P
S = 32
SE = 64
SH = 128
UE = B * FC
UP = 2 * UE
GP = 2 * B
PAIRS = E // 2
LEAD = 3
NZ = 4
NO = 4
NR = 2
NT = 2
SPLIT_AT = 4
LOGITS_AT = 3
EXP_AT = 4
SINE_ARGUMENTS_AT = 7
COMBINE_T_AT = 8
SINES_AT = 9
FIRST_WEIGH_AT = 12
WEIGH_AT = 2

LN_EPS = 1e-5
TIME_EPS = 1e-8
GAMMA_EPS = 1e-8
ROUND = 1.5 * 2.0 ** 23
TWO_PI_HIGH = 6.28125
TWO_PI_LOW = 2 * math.pi - TWO_PI_HIGH


def conditioned_experts_kernel(nc, x, subject_ids, theta, phi, ln_g, ln_b, subj_emb, hyp_w1, hyp_b1,
                               hyp_w2, hyp_b2, sty_w1, sty_b1, sty_w2, sty_b2, router_w, exp_w1,
                               exp_b1, exp_w2, exp_b2, out):
    ctx = ExitStack()
    with ctx:
        def sb(name, shape, dtype=F32):
            return ctx.enter_context(nc.sbuf_tensor(name, shape, dtype))

        def sem(name):
            return ctx.enter_context(nc.semaphore(name))

        x_tok = sb("x_tok", [P, B * TT, P])
        xn_tok = sb("xn_tok", [P, B * TT, P])
        w_raw = sb("w_raw", [P, E, 2 * FF])
        w_hi = [sb(f"w_hi{i}", [P, 2 * FF], F32R) for i in range(2)]
        w_lo = [sb(f"w_lo{i}", [P, 2 * FF], F32R) for i in range(2)]
        b1_now = [sb(f"b1_now{i}", [P, FC]) for i in range(2)]
        h_all = sb("h_all", [P, B, T])
        h_hi = sb("h_hi", [P, B, T], F32R)
        h_lo = sb("h_lo", [P, B, T], F32R)
        hid = [sb(f"hid{i}", [P, T]) for i in range(NR)]
        hid_hi = [sb(f"hid_hi{i}", [P, T], F32R) for i in range(NZ)]
        hid_lo = [sb(f"hid_lo{i}", [P, T], F32R) for i in range(NZ)]
        weighted = [sb(f"weighted{i}", [P, T]) for i in range(NT)]
        y_sum = sb("y_sum", [P, B, T])
        combine_all = sb("combine_all", [P, E, B * T])
        out_tok = sb("out_tok", [P, B, T])

        exp_b_rows = sb("exp_b_rows", [E * FC + E, P])
        exp_b_cols = sb("exp_b_cols", [P, E * FC + E])
        b1_cols = exp_b_cols[:, 0:E * FC]
        b2_cols = exp_b_cols[:, E * FC:E * FC + E]
        ln_cols = sb("ln_cols", [P, 2])
        hyp_b_cols = sb("hyp_b_cols", [P, 2])
        sty_b1_col = sb("sty_b1_col", [SE, 1])
        sty_b2_cols = sb("sty_b2_cols", [P, 2])
        emb = sb("emb", [S, SE])
        hyp_w1_s = sb("hyp_w1_s", [SE, SH])
        hyp_w2_s = sb("hyp_w2_s", [SH, SH])
        sty_w1_s = sb("sty_w1_s", [SH, SH // 2])
        sty_w2_s = sb("sty_w2_s", [SH // 2, 2 * P])
        router_s = sb("router_s", [P, E])
        ids = sb("ids", [S, B], I32)
        ids_f = sb("ids_f", [S, B])
        onehot = sb("onehot", [S, B])
        emb_t = sb("emb_t", [SE, B])
        hyp_1 = sb("hyp_1", [SH, B])
        hyp_2 = sb("hyp_2", [SH, B])
        sty_1 = sb("sty_1", [SH // 2, B])
        gamma = sb("gamma", [P, B])
        beta = sb("beta", [P, B])
        soft = sb("soft", [P, 4 * B])

        stats = sb("stats", [P, B * TT, 6])
        mean_var = sb("mean_var", [P, B * TT, 2])
        tok_s = sb("tok_s", [P, B, 8, TT])
        t_stats = sb("t_stats", [P, B, 6])
        t_mv = sb("t_mv", [P, B, 2])
        t_s = sb("t_s", [P, B, 16])
        g_cols = sb("g_cols", [P, 6])

        part = sb("part", [P, 2], I32)
        part_f = sb("part_f", [P, 4])
        part_odd = sb("part_odd", [P, 1], I32)
        rank_i = sb("rank_i", [P, B * TT, E], I32)
        rank = sb("rank", [P, B * TT, E])
        ident = sb("ident", [P, P])
        above = sb("above", [P, P])
        below = sb("below", [P, P])
        angles = sb("angles", [P, 2, B])
        ang = sb("ang", [P, 12, B])
        rot = sb("rot", [P, B, P])
        rot_t = sb("rot_t", [P, B, P])

        r3 = [P, B * TT, E]
        shifted = sb("shifted", r3)
        e_prob = sb("e_prob", r3)
        prob = sb("prob", r3)
        pick = sb("pick", r3)
        mask1 = sb("mask1", r3)
        rest = sb("rest", r3)
        mask2 = sb("mask2", r3)
        gates = sb("gates", r3)
        combine = sb("combine", r3)
        red = sb("red", [P, 10, B * TT])
        combine_t = sb("combine_t", [E, B * T])
        combine_dram = nc.dram_tensor("combine_dram", (E, B * T), F32, kind="Internal").ap()

        z_ps = [ctx.enter_context(nc.psum_tensor(f"z_ps{i}", [P, T], F32)) for i in range(NZ)]
        o_ps = [ctx.enter_context(nc.psum_tensor(f"o_ps{i}", [P, T], F32)) for i in range(NO)]
        xn_t = [o_ps[0], o_ps[1]]
        x_t = [o_ps[2], o_ps[3]]
        small_ps = z_ps[2]
        bias_ps = z_ps[3]
        logits_ps = o_ps[2]
        combine_ps = [o_ps[2], o_ps[3]]
        final_ps = [[o_ps[0], o_ps[1]], [z_ps[0], z_ps[1]]]

        x_loaded = [sem(f"x_loaded{b}") for b in range(B)]
        subject_loaded = sem("subject_loaded")
        hyp1_loaded = sem("hyp1_loaded")
        hyp2_loaded = sem("hyp2_loaded")
        sty_w_loaded = sem("sty_w_loaded")
        sty_b_loaded = sem("sty_b_loaded")
        ln_loaded = sem("ln_loaded")
        exp_b_loaded = sem("exp_b_loaded")
        router_loaded = sem("router_loaded")
        angles_loaded = sem("angles_loaded")
        w_first_loaded = sem("w_first_loaded")
        w_second_loaded = sem("w_second_loaded")
        w_rest_loaded = sem("w_rest_loaded")
        combine_stored = sem("combine_stored")
        cb_first_loaded = sem("cb_first_loaded")
        cb_second_loaded = sem("cb_second_loaded")
        cb_rest_loaded = sem("cb_rest_loaded")
        out_stored = sem("out_stored")
        consts_ready = sem("consts_ready")
        onehot_step = sem("onehot_step")
        subject_mm = sem("subject_mm")
        subject_act = sem("subject_act")
        soft_step = sem("soft_step")
        bias_t = sem("bias_t")
        bias_ready = sem("bias_ready")
        style_ready = sem("style_ready")
        tok_var = sem("tok_var")
        tok_seed = sem("tok_seed")
        xn_ready = sem("xn_ready")
        xn_t_ready = sem("xn_t_ready")
        x_t_ready = sem("x_t_ready")
        y_init = sem("y_init")
        t_var = sem("t_var")
        t_seed = sem("t_seed")
        affine_ready = sem("affine_ready")
        h_ready = sem("h_ready")
        h_hi_ready = sem("h_hi_ready")
        h_lo_ready = sem("h_lo_ready")
        logits_ready = sem("logits_ready")
        shifted_ready = sem("shifted_ready")
        e_prob_ready = sem("e_prob_ready")
        combine_ready = sem("combine_ready")
        combine_t_ps = sem("combine_t_ps")
        combine_t_ready = sem("combine_t_ready")
        angles_ready = sem("angles_ready")
        sines_ready = sem("sines_ready")
        rot_ready = sem("rot_ready")
        dve_step = sem("dve_step")
        w_hi_ready = sem("w_hi_ready")
        w_lo_ready = sem("w_lo_ready")
        z_ready = sem("z_ready")
        hid_ready = sem("hid_ready")
        hi_by_act = sem("hi_by_act")
        hi_by_dve = sem("hi_by_dve")
        lo_ready = sem("lo_ready")
        unit_done = sem("unit_done")
        weighted_ready = sem("weighted_ready")
        y_added = sem("y_added")
        final_ready = sem("final_ready")
        out_by_act = sem("out_by_act")
        out_by_dve = sem("out_by_dve")
        b1_copied = sem("b1_copied")

        block = ctx.enter_context(nc.Block())
        HALF = T // 2

        @block.sync
        def _(sp):
            for b in range(B):
                sp.dma_start(x_tok[:, b * TT:(b + 1) * TT, :],
                             x[b].rearrange("(p t) d -> p t d", t=TT)).then_inc(x_loaded[b], 16)
            for e in range(E):
                loaded = w_first_loaded if e == 0 else w_second_loaded if e == 1 else w_rest_loaded
                sp.dma_start(w_raw[:, e, 0:FF], exp_w1[e]).then_inc(loaded, 16)
                sp.dma_start(w_raw[:, e, FF:2 * FF].rearrange("p (c d) -> p c d", c=FC),
                             exp_w2[e].rearrange("(c p) d -> p c d", p=P)).then_inc(loaded, 16)
            sp.wait_ge(combine_t_ready, B)
            sp.dma_start(combine_dram, combine_t[:, :]).then_inc(combine_stored, 16)
            sp.wait_ge(combine_stored, 16)
            for e in range(E):
                loaded = cb_first_loaded if e == 0 else cb_second_loaded if e == 1 else cb_rest_loaded
                sp.dma_start(combine_all[:, e, :],
                             combine_dram[e:e + 1, :].to_broadcast([P, B * T])).then_inc(loaded, 16)
            for b in range(B):
                out_b = out[b].rearrange("(p t) d -> p (t d)", t=TT)
                sp.wait_ge(out_by_act, b + 1)
                sp.dma_start(out_b[:, 0:HALF], out_tok[:, b, 0:HALF]).then_inc(out_stored, 16)
            sp.wait_ge(out_stored, 2 * B * 16)

        @block.gpsimd
        def _(pool):
            pool.dma_start(sty_w1_s[:, :], sty_w1).then_inc(sty_w_loaded, 16)
            pool.dma_start(sty_w2_s[:, :], sty_w2).then_inc(sty_w_loaded, 16)
            nc.gpsimd.iota(part[:, 0:1], [[0, 1]], base=0, channel_multiplier=1).then_inc(consts_ready, 1)
            nc.gpsimd.memset(ident[:, :], 0.0).then_inc(consts_ready, 1)
            pool.wait_ge(consts_ready, 2)
            nc.gpsimd.affine_select(out=ident[:, :], in_=ident[:, :], compare_op=ALU.not_equal, fill=1.0,
                                    base=0, pattern=[[-1, P]], channel_multiplier=1).then_inc(consts_ready, 1)
            nc.gpsimd.tensor_copy(part_f[:, 0:1], part[:, 0:1]).then_inc(consts_ready, 1)
            pool.wait_ge(subject_loaded, 32)
            nc.gpsimd.tensor_scalar(ids_f[:, :], ids[:, :], float(S - 1), 0.0, ALU.min, ALU.max)\
                .then_inc(onehot_step, 1)
            pool.wait_ge(onehot_step, 1)
            pool.wait_ge(consts_ready, 4)
            nc.gpsimd.tensor_scalar(onehot[:, :], ids_f[:, :], part_f[0:S, 0:1], None, ALU.is_equal)\
                .then_inc(onehot_step, 1)
            pool.dma_start(exp_b_rows[0:E * FC, :], exp_b1.rearrange("e (c p) -> (e c) p", p=P))\
                .then_inc(exp_b_loaded, 16)
            pool.dma_start(exp_b_rows[E * FC:E * FC + E, :], exp_b2).then_inc(exp_b_loaded, 16)
            pool.dma_start(router_s[:, :], router_w).then_inc(router_loaded, 16)
            for n, a in enumerate((theta, phi)):
                pool.dma_start(angles[:, n, :], a.rearrange("(o b) -> o b", o=1).to_broadcast([P, B]))\
                    .then_inc(angles_loaded, 16)
            nc.gpsimd.iota(rank_i[:, :, :], [[0, B * TT], [-1, E]], base=E, channel_multiplier=0)\
                .then_inc(consts_ready, 1)
            for m in (above, below):
                nc.gpsimd.memset(m[:, :], 0.0).then_inc(consts_ready, 1)
            for n, (m, base) in enumerate(((above, 1), (below, -1))):
                pool.wait_ge(consts_ready, 6 + n)
                nc.gpsimd.affine_select(out=m[:, :], in_=m[:, :], compare_op=ALU.not_equal, fill=1.0,
                                        base=base, pattern=[[-1, P]], channel_multiplier=1)\
                    .then_inc(consts_ready, 1)

            def split_low(i, k):
                for half in range(2):
                    cols = slice(half * FF, (half + 1) * FF)
                    pool.wait_ge(w_hi_ready, 4 * i + 2 * k + half + 1)
                    nc.gpsimd.tensor_tensor(w_lo[k % 2][:, cols], w_raw[:, 2 * i + k, cols],
                                            w_hi[k % 2][:, cols].bitcast(F32), ALU.subtract)\
                        .then_inc(w_lo_ready, 1)

            def add_group(i, q):
                pool.wait_ge(weighted_ready, GP * i + q + 1)
                b = q % B
                if isinstance(i, int) and GP * i + q < B:
                    pool.wait_ge(y_init, b + 1)
                else:
                    pool.wait_ge(y_added, GP * i + q - B + 1)
                nc.gpsimd.tensor_tensor(y_sum[:, b, :], y_sum[:, b, :], weighted[q % NT][:, :], ALU.add)\
                    .then_inc(y_added, 1)

            def pair(i, first=False, last=False):
                if not first:
                    add_group(i, -1)
                split_low(i, 1)
                add_group(i, 0)
                add_group(i, 1)
                if not last:
                    split_low(i, 2)
                    add_group(i, 2)

            split_low(0, 0)
            pair(0, first=True)
            with pool.Fori(1, PAIRS - 1) as i:
                pair(i)
            pair(PAIRS - 1, last=True)

        @block.scalar
        def _(act):
            nc.scalar.preload_act_table_set("natural_log_exp_and_others")
            act.dma_start(ids[:, :], subject_ids.rearrange("(o b) -> o b", o=1).to_broadcast([S, B]))\
                .then_inc(subject_loaded, 16)
            act.dma_start(emb[:, :], subj_emb).then_inc(subject_loaded, 16)
            act.dma_start(hyp_w1_s[:, :], hyp_w1).then_inc(hyp1_loaded, 16)
            act.dma_start(hyp_b_cols[:, 0:1], hyp_b1.rearrange("(p o) -> p o", o=1)).then_inc(hyp1_loaded, 16)
            act.dma_start(hyp_w2_s[:, :], hyp_w2).then_inc(hyp2_loaded, 16)
            act.dma_start(hyp_b_cols[:, 1:2], hyp_b2.rearrange("(p o) -> p o", o=1)).then_inc(hyp2_loaded, 16)
            act.dma_start(ln_cols[:, 0:1], ln_g.rearrange("(p o) -> p o", o=1)).then_inc(ln_loaded, 16)
            act.dma_start(ln_cols[:, 1:2], ln_b.rearrange("(p o) -> p o", o=1)).then_inc(ln_loaded, 16)
            act.dma_start(sty_b1_col[:, :], sty_b1.rearrange("(p o) -> p o", o=1)).then_inc(sty_b_loaded, 16)
            for n in range(2):
                act.dma_start(sty_b2_cols[:, n:n + 1], sty_b2[n * P:(n + 1) * P].rearrange("(p o) -> p o", o=1))\
                    .then_inc(sty_b_loaded, 16)

            def seed(b):
                act.wait_ge(tok_var, b + 1)
                nc.scalar.activation(tok_s[:, b, 1, :], tok_s[:, b, 0, :], ACT.Ln).then_inc(tok_seed, 1)
                act.wait_ge(tok_seed, 2 * b + 1)
                nc.scalar.activation(tok_s[:, b, 2, :], tok_s[:, b, 1, :], ACT.Exp, scale=-0.5)\
                    .then_inc(tok_seed, 1)

            act.wait_ge(subject_mm, 1)
            nc.scalar.copy(emb_t[:, :], small_ps[0:SE, 0:B]).then_inc(subject_act, 1)
            seed(0)
            act.wait_ge(subject_mm, 2)
            nc.scalar.activation(hyp_1[:, :], small_ps[:, 2:2 + B], ACT.Relu, bias=hyp_b_cols[:, 0:1])\
                .then_inc(subject_act, 1)
            seed(1)
            act.wait_ge(subject_mm, 3)
            nc.scalar.activation(hyp_2[:, :], small_ps[:, 4:4 + B], ACT.Identity, bias=hyp_b_cols[:, 1:2])\
                .then_inc(subject_act, 1)
            act.wait_ge(subject_mm, 4)
            act.wait_ge(sty_b_loaded, 48)
            nc.scalar.activation(sty_1[:, :], small_ps[0:SH // 2, 6:6 + B], ACT.Relu, bias=sty_b1_col[:, :])\
                .then_inc(subject_act, 1)
            act.wait_ge(subject_mm, 5)
            graw, braw = small_ps[:, 8:8 + B], small_ps[:, 10:10 + B]
            bias = sty_b2_cols[:, 0:1]
            nc.scalar.activation(soft[:, 0:B], graw, ACT.Abs, bias=bias).then_inc(soft_step, 1)
            nc.scalar.activation(soft[:, 3 * B:4 * B], graw, ACT.Relu, bias=bias).then_inc(soft_step, 1)
            act.wait_ge(soft_step, 1)
            nc.scalar.activation(soft[:, B:2 * B], soft[:, 0:B], ACT.Exp, scale=-1.0).then_inc(soft_step, 1)
            act.wait_ge(soft_step, 3)
            nc.scalar.activation(soft[:, 2 * B:3 * B], soft[:, B:2 * B], ACT.Ln, bias=1.0).then_inc(soft_step, 1)
            nc.scalar.activation(beta[:, :], braw, ACT.Identity, bias=sty_b2_cols[:, 1:2]).then_inc(soft_step, 1)
            act.wait_ge(bias_t, 1)
            nc.scalar.copy(exp_b_cols[:, :], bias_ps[:, 0:E * FC + E]).then_inc(bias_ready, 1)


            def split_high(i, k, half):
                cols = slice(half * FF, (half + 1) * FF)
                if half == 0:
                    nc.scalar.copy(b1_now[k % 2][:, :], b1_cols[:, bass.ds((2 * i + k) * FC, FC)])\
                        .then_inc(b1_copied, 1)
                nc.scalar.activation(w_hi[k % 2][:, cols], w_raw[:, 2 * i + k, cols], ACT.Copy)\
                    .then_inc(w_hi_ready, 1)

            def hidden(i, k, first):
                u = UP * i + k
                bias = b1_now[k // UE][:, k % FC:k % FC + 1]
                act.wait_ge(z_ready, u + 1)
                if k % 2 == 0:
                    if not (first and k < NZ):
                        act.wait_ge(unit_done, u - NZ + 1)
                    nc.scalar.activation(hid_hi[k % NZ][:, :], z_ps[k % NZ][:, :], ACT.Relu, bias=bias)\
                        .then_inc(hi_by_act, 1)
                if not (first and k < NR):
                    act.wait_ge(lo_ready, u - NR + 1)
                nc.scalar.activation(hid[k % NR][:, :], z_ps[k % NZ][:, :], ACT.Relu, bias=bias)\
                    .then_inc(hid_ready, 1)

            act.wait_ge(w_first_loaded, 32)
            act.wait_ge(bias_ready, 1)
            for b in range(B):
                split_high(0, 0, b)
                act.wait_ge(t_var, b + 1)
                nc.scalar.activation(t_s[:, b, 1:2], t_s[:, b, 0:1], ACT.Ln).then_inc(t_seed, 1)
                act.wait_ge(t_seed, 2 * b + 1)
                nc.scalar.activation(t_s[:, b, 2:3], t_s[:, b, 1:2], ACT.Exp, scale=-0.5).then_inc(t_seed, 1)
            for b in range(B):
                act.wait_ge(affine_ready, 2 * (b + 1))
                nc.scalar.activation(h_all[:, b, :], xn_t[b][:, :], ACT.Identity, scale=t_s[:, b, 8:9],
                                     bias=t_s[:, b, 10:11]).then_inc(h_ready, 1)
            for b in range(B):
                act.wait_ge(x_t_ready, b + 1)
                nc.scalar.copy(y_sum[:, b, :], x_t[b][:, :]).then_inc(y_init, 1)

            def exponentials():
                act.wait_ge(shifted_ready, 1)
                nc.scalar.activation(e_prob[:, :, :], shifted[:, :, :], ACT.Exp).then_inc(e_prob_ready, 1)

            def combine_columns():
                for b in range(B):
                    act.wait_ge(combine_t_ps, b + 1)
                    nc.scalar.copy(combine_t[:, b * T:(b + 1) * T], combine_ps[b][0:E, :])\
                        .then_inc(combine_t_ready, 1)

            def sines():
                act.wait_ge(angles_ready, 1)
                nc.scalar.activation(ang[:, 6, :], ang[:, 4, :], ACT.Sin).then_inc(sines_ready, 1)
                nc.scalar.activation(ang[:, 7, :], ang[:, 5, :], ACT.Sin).then_inc(sines_ready, 1)

            extra = {EXP_AT: exponentials, COMBINE_T_AT: combine_columns, SINES_AT: sines}

            def pair(i, first=False, last=False):
                for k in range(UP):
                    if k % UE == 0:
                        act.wait_ge(b1_copied, 2 * i + k // UE + 1)
                    hidden(i, k, first)
                    if first and k in extra:
                        extra[k]()
                    half = k % UE - SPLIT_AT
                    if half in (0, 1) and not (last and k >= UE):
                        if first and half == 0:
                            if k < UE:
                                act.wait_ge(w_second_loaded, 32)
                            else:
                                act.wait_ge(w_rest_loaded, (E - 2) * 32)
                        split_high(i, k // UE + 1, half)

            pair(0, first=True)
            with act.Fori(1, PAIRS - 1) as i:
                pair(i)
            pair(PAIRS - 1, last=True)
            for b in range(B):
                act.wait_ge(final_ready, b + 1)
                nc.scalar.copy(out_tok[:, b, 0:HALF], final_ps[b][0][:, 0:HALF]).then_inc(out_by_act, 1)
            for b in range(B):
                out_b = out[b].rearrange("(p t) d -> p (t d)", t=TT)
                act.wait_ge(out_by_dve, b + 1)
                act.dma_start(out_b[:, HALF:T], out_tok[:, b, HALF:T]).then_inc(out_stored, 16)

        @block.vector
        def _(dve):
            done = [0]

            def step(ins):
                done[0] += 1
                ins.then_inc(dve_step, 1)
                return done[0]

            def settle(ins):
                dve.wait_ge(dve_step, step(ins))

            def token_stats(b):
                dve.wait_ge(x_loaded[b], 16)
                for t in range(TT):
                    n = step(nc.vector.bn_stats(stats[:, b * TT + t, :], x_tok[:, b * TT + t, :]))
                for t in range(TT):
                    dve.wait_ge(dve_step, n - TT + 1 + t)
                    m = step(nc.vector.bn_aggr(mean_var[:, b * TT + t, :], stats[:, b * TT + t, :]))
                dve.wait_ge(dve_step, m)
                nc.vector.tensor_scalar(tok_s[:, b, 0, :], mean_var[:, b * TT:(b + 1) * TT, 1], LN_EPS, None,
                                        ALU.add).then_inc(tok_var, 1)

            def refine(y, v, a, c, r):
                settle(nc.vector.tensor_tensor(a, y, y, ALU.mult))
                settle(nc.vector.tensor_tensor(c, a, v, ALU.mult))
                settle(nc.vector.tensor_scalar(a, c, -0.5, 1.5, ALU.mult, ALU.add))
                settle(nc.vector.tensor_tensor(r, y, a, ALU.mult))

            def normalise(b):
                s = tok_s[:, b, :, :]
                dve.wait_ge(tok_seed, 2 * (b + 1))
                refine(s[:, 2, :], s[:, 0, :], s[:, 3, :], s[:, 4, :], s[:, 5, :])
                for t in range(TT):
                    nc.vector.tensor_scalar(xn_tok[:, b * TT + t, :], x_tok[:, b * TT + t, :],
                                            mean_var[:, b * TT + t, 0:1], s[:, 5, t:t + 1],
                                            ALU.subtract, ALU.mult).then_inc(xn_ready, 1)

            def time_stats(b):
                dve.wait_ge(xn_t_ready, b + 1)
                settle(nc.vector.bn_stats(t_stats[:, b, :], xn_t[b][:, :]))
                settle(nc.vector.bn_aggr(t_mv[:, b, :], t_stats[:, b, :]))
                nc.vector.tensor_scalar(t_s[:, b, 0:1], t_mv[:, b, 1:2], g_cols[:, 0:1], TIME_EPS,
                                        ALU.mult, ALU.add).then_inc(t_var, 1)
                settle(nc.vector.tensor_scalar(t_s[:, b, 6:7], t_mv[:, b, 0:1], ln_cols[:, 0:1], ln_cols[:, 1:2],
                                               ALU.mult, ALU.add))
                dve.wait_ge(style_ready, 3)
                settle(nc.vector.tensor_scalar(t_s[:, b, 7:8], t_s[:, b, 6:7], ln_cols[:, 1:2],
                                               g_cols[:, 4 + b:5 + b], ALU.subtract, ALU.mult))

            def affine(b):
                s = t_s[:, b, :]
                dve.wait_ge(t_seed, 2 * (b + 1))
                refine(s[:, 2:3], s[:, 0:1], s[:, 3:4], s[:, 4:5], s[:, 5:6])
                nc.vector.tensor_scalar(s[:, 8:9], s[:, 5:6], g_cols[:, 2 + b:3 + b], None, ALU.mult)\
                    .then_inc(affine_ready, 1)
                dve.wait_ge(soft_step, 5)
                nc.vector.tensor_scalar(s[:, 10:11], s[:, 7:8], s[:, 5:6], beta[:, b:b + 1], ALU.mult, ALU.add)\
                    .then_inc(affine_ready, 1)

            def split_h(b):
                dve.wait_ge(h_ready, b + 1)
                nc.vector.tensor_copy(h_hi[:, b, :], h_all[:, b, :]).then_inc(h_hi_ready, 1)
                dve.wait_ge(h_hi_ready, b + 1)
                nc.vector.tensor_tensor(h_lo[:, b, :], h_all[:, b, :], h_hi[:, b, :].bitcast(F32), ALU.subtract)\
                    .then_inc(h_lo_ready, 1)

            token_stats(0)
            token_stats(1)
            normalise(0)
            normalise(1)
            dve.wait_ge(ln_loaded, 32)
            settle(nc.vector.tensor_tensor(g_cols[:, 0:1], ln_cols[:, 0:1], ln_cols[:, 0:1], ALU.mult))
            dve.wait_ge(soft_step, 4)
            nc.vector.tensor_tensor(soft[:, 0:B], soft[:, 2 * B:3 * B], soft[:, 3 * B:4 * B], ALU.add)\
                .then_inc(style_ready, 1)
            dve.wait_ge(style_ready, 1)
            settle(nc.vector.tensor_scalar(gamma[:, :], soft[:, 0:B], GAMMA_EPS, None, ALU.add))
            nc.vector.tensor_scalar(g_cols[:, 2:4], gamma[:, :], ln_cols[:, 0:1], None, ALU.mult)\
                .then_inc(style_ready, 1)
            nc.vector.tensor_scalar(g_cols[:, 4:6], gamma[:, :], -1.0, None, ALU.mult).then_inc(style_ready, 1)
            time_stats(0)
            time_stats(1)
            affine(0)
            affine(1)
            split_h(0)
            split_h(1)

            def over(m):
                return red[:, m, :].unsqueeze(2).to_broadcast([P, B * TT, E])

            def reduce(m, src, op):
                settle(nc.vector.tensor_reduce(red[:, m, :], src[:, :, :], axis=AX_X, op=op))

            def tt(o, a, b_, op):
                settle(nc.vector.tensor_tensor(o[:, :, :], a[:, :, :], b_, op))

            def first_at(m, src, mask):
                reduce(m, src, ALU.max)
                tt(pick, src, over(m), ALU.is_equal)
                tt(pick, pick, rank[:, :, :], ALU.mult)
                reduce(m + 1, pick, ALU.max)
                tt(mask, rank, over(m + 1), ALU.is_equal)

            def route_a():
                dve.wait_ge(consts_ready, 5)
                settle(nc.vector.tensor_copy(rank[:, :, :], rank_i[:, :, :]))
                dve.wait_ge(logits_ready, B)
                settle(nc.vector.tensor_reduce(red[:, 0, :], logits_ps[:, 0:B * TT * E].rearrange("p (j e) -> p j e", e=E), axis=AX_X, op=ALU.max))
                nc.vector.tensor_tensor(shifted[:, :, :], logits_ps[:, 0:B * TT * E].rearrange("p (j e) -> p j e", e=E), over(0), ALU.subtract)\
                    .then_inc(shifted_ready, 1)

            def route_b():
                dve.wait_ge(e_prob_ready, 1)
                reduce(1, e_prob, ALU.add)
                settle(nc.vector.reciprocal(red[:, 2, :], red[:, 1, :]))
                tt(prob, e_prob, over(2), ALU.mult)
                first_at(3, prob, mask1)

            def route_c():
                settle(nc.vector.scalar_tensor_tensor(rest[:, :, :], mask1[:, :, :], -2.0, prob[:, :, :],
                                                      ALU.mult, ALU.add))
                first_at(5, rest, mask2)
                tt(mask1, mask1, mask2[:, :, :], ALU.add)
                tt(gates, prob, mask1[:, :, :], ALU.mult)
                reduce(7, gates, ALU.add)
                settle(nc.vector.reciprocal(red[:, 8, :], red[:, 7, :]))
                nc.vector.tensor_tensor(combine[:, :, :], gates[:, :, :], over(8), ALU.mult)\
                    .then_inc(combine_ready, 1)

            def sine_arguments():
                dve.wait_ge(angles_loaded, 32)
                dve.wait_ge(consts_ready, 4)
                settle(nc.vector.tensor_scalar(part[:, 1:2], part[:, 0:1], 2, None, ALU.bitwise_and))
                settle(nc.vector.tensor_scalar(part_odd[:, :], part[:, 0:1], 1, None, ALU.bitwise_and))
                settle(nc.vector.tensor_scalar(part_f[:, 1:2], part[:, 1:2], 0.5, None, ALU.mult))
                settle(nc.vector.tensor_scalar(part_f[:, 2:3], part_f[:, 1:2], -1.0, 1.0, ALU.mult, ALU.add))
                settle(nc.vector.tensor_copy(part_f[:, 3:4], part_odd[:, :]))
                settle(nc.vector.tensor_scalar(ang[:, 0, :], angles[:, 0, :], part_f[:, 2:3], None, ALU.mult))
                settle(nc.vector.scalar_tensor_tensor(ang[:, 1, :], angles[:, 1, :], part_f[:, 1:2], ang[:, 0, :],
                                                      ALU.mult, ALU.add))
                settle(nc.vector.tensor_scalar(ang[:, 2, :], ang[:, 1, :], 1 / (2 * math.pi), ROUND,
                                               ALU.mult, ALU.add))
                settle(nc.vector.tensor_scalar(ang[:, 3, :], ang[:, 2, :], -ROUND, None, ALU.add))
                settle(nc.vector.scalar_tensor_tensor(ang[:, 4, :], ang[:, 3, :], -TWO_PI_HIGH, ang[:, 1, :],
                                                      ALU.mult, ALU.add))
                settle(nc.vector.scalar_tensor_tensor(ang[:, 5, :], ang[:, 3, :], -TWO_PI_LOW, ang[:, 4, :],
                                                      ALU.mult, ALU.add))
                pi = 3.1415925
                settle(nc.vector.tensor_scalar(ang[:, 4, :], ang[:, 5, :], pi, -pi, ALU.min, ALU.max))
                settle(nc.vector.tensor_scalar(ang[:, 8, :], ang[:, 4, :], -1.0, None, ALU.mult))
                settle(nc.vector.tensor_tensor(ang[:, 9, :], ang[:, 4, :], ang[:, 8, :], ALU.max))
                nc.vector.tensor_scalar(ang[:, 5, :], ang[:, 9, :], -1.0, math.pi / 2, ALU.mult, ALU.add)\
                    .then_inc(angles_ready, 1)

            def rotations():
                dve.wait_ge(sines_ready, 1)
                dve.wait_ge(consts_ready, 9)
                settle(nc.vector.tensor_scalar(ang[:, 0, :], ang[:, 6, :], part_f[:, 3:4], None, ALU.mult))
                settle(nc.vector.tensor_tensor(ang[:, 1, :], ang[:, 0, :], ang[:, 6, :], ALU.subtract))
                for b in range(B):
                    settle(nc.vector.tensor_scalar(rot_t[:, b, :], ident[:, :], ang[:, 7, b:b + 1], None, ALU.mult))
                for b in range(B):
                    settle(nc.vector.scalar_tensor_tensor(rot[:, b, :], below[:, :], ang[:, 0, b:b + 1],
                                                          rot_t[:, b, :], ALU.mult, ALU.add))
                for b in range(B):
                    settle(nc.vector.scalar_tensor_tensor(rot_t[:, b, :], above[:, :], ang[:, 1, b:b + 1],
                                                          rot[:, b, :], ALU.mult, ALU.add))
                for b in range(B):
                    nc.vector.tensor_copy(rot[:, b, :], rot_t[:, b, :]).then_inc(rot_ready, 1)

            extra = {LOGITS_AT: route_a, EXP_AT: route_b, EXP_AT + 1: route_c, SINE_ARGUMENTS_AT: sine_arguments,
                     SINES_AT + 1: rotations}

            def split_unit(i, k, first):
                dve.wait_ge(hid_ready, UP * i + k + 1)
                if not (first and k < NZ):
                    dve.wait_ge(unit_done, UP * i + k - NZ + 1)
                if k % 2 == 1:
                    nc.vector.tensor_copy(hid_hi[k % NZ][:, :], hid[k % NR][:, :]).then_inc(hi_by_dve, 1)
                    dve.wait_ge(hi_by_dve, UP // 2 * i + (k + 1) // 2)
                nc.vector.tensor_tensor(hid_lo[k % NZ][:, :], hid[k % NR][:, :],
                                        hid_hi[k % NZ][:, :].bitcast(F32), ALU.subtract).then_inc(lo_ready, 1)

            def weigh_group(i, q, first=False):
                b, e = q % B, 2 * i + q // B
                dve.wait_ge(unit_done, UP * i + (q + 1) * FC)
                if not (first and q < NT):
                    dve.wait_ge(y_added, GP * i + q - NT + 1)
                nc.vector.scalar_tensor_tensor(weighted[q % NT][:, :], o_ps[q % NO][:, :],
                                               b2_cols[:, bass.ds(e, 1)],
                                               combine_all[:, e, b * T:(b + 1) * T], ALU.add, ALU.mult)\
                    .then_inc(weighted_ready, 1)

            first_weighed = {FIRST_WEIGH_AT: 0, FIRST_WEIGH_AT + 1: 1, UP - FC + WEIGH_AT: 2}
            for k in range(UP):
                split_unit(0, k, first=True)
                if k in extra:
                    extra[k]()
                if k in first_weighed:
                    q = first_weighed[k]
                    if q == 0:
                        dve.wait_ge(cb_first_loaded, 16)
                    if q == B:
                        dve.wait_ge(cb_second_loaded, 16)
                    weigh_group(0, q, first=True)
            dve.wait_ge(cb_rest_loaded, (E - 2) * 16)
            with dve.Fori(1, PAIRS) as i:
                for k in range(UP):
                    split_unit(i, k, first=False)
                    if k % FC == WEIGH_AT:
                        weigh_group(i, k // FC - 1)
            weigh_group(PAIRS, -1)
            for b in range(B):
                dve.wait_ge(final_ready, b + 1)
                nc.vector.tensor_copy(out_tok[:, b, HALF:T], final_ps[b][1][:, 0:HALF]).then_inc(out_by_dve, 1)

        @block.tensor
        def _(pe):
            def mm(o, l, r, start=True, stop=True):
                return nc.tensor.matmul(o, l, r, start=start, stop=stop)

            def transposed(o, i, n=P):
                return nc.tensor.transpose(o, i, ident[0:n, 0:n])

            pe.wait_ge(onehot_step, 2)
            pe.wait_ge(subject_loaded, 32)
            mm(small_ps[0:SE, 0:B], emb[:, :], onehot[:, :]).then_inc(subject_mm, 1)
            pe.wait_ge(hyp1_loaded, 32)
            pe.wait_ge(subject_act, 1)
            mm(small_ps[:, 2:2 + B], hyp_w1_s[:, :], emb_t[:, :]).then_inc(subject_mm, 1)
            pe.wait_ge(consts_ready, 4)
            for b in range(B):
                pe.wait_ge(x_loaded[b], 16)
                for t in range(TT):
                    m = transposed(x_t[b][:, t * P:(t + 1) * P], x_tok[:, b * TT + t, :])
                m.then_inc(x_t_ready, 1)
            pe.wait_ge(hyp2_loaded, 32)
            pe.wait_ge(subject_act, 2)
            mm(small_ps[:, 4:4 + B], hyp_w2_s[:, :], hyp_1[:, :]).then_inc(subject_mm, 1)
            pe.wait_ge(sty_w_loaded, 32)
            pe.wait_ge(subject_act, 3)
            mm(small_ps[0:SH // 2, 6:6 + B], sty_w1_s[:, :], hyp_2[:, :]).then_inc(subject_mm, 1)
            pe.wait_ge(subject_act, 4)
            mm(small_ps[:, 8:8 + B], sty_w2_s[:, 0:P], sty_1[:, :])
            mm(small_ps[:, 10:10 + B], sty_w2_s[:, P:2 * P], sty_1[:, :]).then_inc(subject_mm, 1)
            for b in range(B):
                for t in range(TT):
                    pe.wait_ge(xn_ready, b * TT + t + 1)
                    m = transposed(xn_t[b][:, t * P:(t + 1) * P], xn_tok[:, b * TT + t, :])
                m.then_inc(xn_t_ready, 1)
            pe.wait_ge(exp_b_loaded, 32)
            transposed(bias_ps[:, 0:E * FC + E], exp_b_rows[:, :], E * FC + E).then_inc(bias_t, 1)

            def first_product(i, k, first):
                parity, b, c = k // UE, k // FC % B, k % FC
                if k % UE == 0:
                    pe.wait_ge(w_lo_ready, 4 * i + 2 * parity + 1)
                if not (first and k < NZ):
                    pe.wait_ge(hid_ready, UP * i + k - NZ + 1)
                elif k == 2:
                    pe.wait_ge(soft_step, 5)
                elif k == 3:
                    pe.wait_ge(bias_ready, 1)
                z = z_ps[k % NZ][:, :]
                cols = slice(c * P, (c + 1) * P)
                if first and k in (0, FC):
                    pe.wait_ge(h_hi_ready, b + 1)
                mm(z, w_hi[parity][:, cols], h_hi[:, b, :], True, False)
                mm(z, w_lo[parity][:, cols], h_hi[:, b, :], False, False)
                if first and k in (0, FC):
                    pe.wait_ge(h_lo_ready, b + 1)
                mm(z, w_hi[parity][:, cols], h_lo[:, b, :], False, True).then_inc(z_ready, 1)

            def second_product(i, k, first=False):
                parity, c = k // UE % 2, k % FC
                if k % UE == 0:
                    pe.wait_ge(w_lo_ready, 4 * i + 2 * parity + 2)
                if c == 0:
                    if not first:
                        pe.wait_ge(weighted_ready, GP * i + k // FC - NO + 1)
                    elif k >= 2 * FC:
                        pe.wait_ge(combine_t_ready, k // FC - 1)
                o = o_ps[k // FC % NO][:, :]
                cols = slice(FF + c * P, FF + (c + 1) * P)
                pe.wait_ge(hi_by_act if k % 2 == 0 else hi_by_dve, UP // 2 * i + k // 2 + 1)
                mm(o, w_hi[parity][:, cols], hid_hi[k % NZ][:, :], c == 0, False)
                mm(o, w_lo[parity][:, cols], hid_hi[k % NZ][:, :], False, False)
                pe.wait_ge(lo_ready, UP * i + k + 1)
                mm(o, w_hi[parity][:, cols], hid_lo[k % NZ][:, :], False, c == FC - 1).then_inc(unit_done, 1)

            def logits(b):
                if b == 0:
                    pe.wait_ge(router_loaded, 16)
                    pe.wait_ge(y_init, 1)
                pe.wait_ge(h_ready, b + 1)
                for j in range(b * TT, (b + 1) * TT):
                    m = mm(logits_ps[:, j * E:(j + 1) * E], h_all[:, b, (j % TT) * P:(j % TT + 1) * P],
                           router_s[:, :])
                m.then_inc(logits_ready, 1)

            def combine_transposes():
                pe.wait_ge(combine_ready, 1)
                pe.wait_ge(y_init, B)
                for b in range(B):
                    for t in range(TT):
                        m = transposed(combine_ps[b][0:E, t * P:(t + 1) * P], combine[:, b * TT + t, :])
                    m.then_inc(combine_t_ps, 1)

            for k in range(UP):
                first_product(0, k, first=True)
                if k in (FC - 2, FC):
                    logits(k // FC)
                if k >= LEAD:
                    second_product(0, k - LEAD, first=True)
                if k == COMBINE_T_AT - 1:
                    combine_transposes()
            with pe.Fori(1, PAIRS) as i:
                for k in range(UP):
                    first_product(i, k, first=False)
                    second_product(i, k - LEAD)
            for k in range(-LEAD, 0):
                second_product(PAIRS, k)

            pe.wait_ge(rot_ready, B)
            pe.wait_ge(weighted_ready, E * B - B)
            pe.wait_ge(hid_ready, E * UE)
            HT = TT // 2
            for b in range(B):
                pe.wait_ge(y_added, E * B - 2 * B + b + 1)
                for t in range(TT):
                    mm(final_ps[b][t // HT][:, t % HT * P:(t % HT + 1) * P], y_sum[:, b, t * P:(t + 1) * P],
                       rot[:, b, :], t % HT == 0, False)
                pe.wait_ge(weighted_ready, E * B - B + b + 1)
                for t in range(TT):
                    m = mm(final_ps[b][t // HT][:, t % HT * P:(t % HT + 1) * P],
                           weighted[b][:, t * P:(t + 1) * P], rot[:, b, :], False, t % HT == HT - 1)
                m.then_inc(final_ready, 1)


_INS = ["x", "itok_B_6_14", "condB_theta", "condB_phi", "L0_cond_ln_g", "L0_cond_ln_b", "L0_cond_subj_emb",
        "L0_cond_hyp_w1", "L0_cond_hyp_b1", "L0_cond_hyp_w2", "L0_cond_hyp_b2", "L0_cond_sty_w1",
        "L0_cond_sty_b1", "L0_cond_sty_w2", "L0_cond_sty_b2", "L0_cond_router_w", "L0_cond_exp_w1",
        "L0_cond_exp_b1", "L0_cond_exp_w2", "L0_cond_exp_b2"]


def kernel(**inputs):
    import numpy as np
    import concourse.bacc as bacc
    from concourse.bass_utils import run_bass_kernel_spmd

    nc = bacc.Bacc("TRN2", target_bir_lowering=False, num_devices=1)
    arrays, args = {}, []
    for name in _INS:
        a = np.ascontiguousarray(inputs[name])
        arrays[f"in_{name}_dram"] = a
        args.append(nc.dram_tensor(f"in_{name}_dram", a.shape, mybir.dt.from_np(a.dtype), kind="ExternalInput").ap())
    out = nc.dram_tensor("out_dram", (B, T, P), F32, kind="ExternalOutput").ap()
    conditioned_experts_kernel(nc, *args, out)
    return run_bass_kernel_spmd(nc, [arrays], core_ids=[0]).results[0]["out_dram"]
```

```python
import math
from contextlib import ExitStack

import concourse.bass as bass
from concourse import mybir

ALU = mybir.AluOpType
ACT = mybir.ActivationFunctionType
AX_X = mybir.AxisListType.X
F32 = mybir.dt.float32
F32R = mybir.dt.float32r
I32 = mybir.dt.int32

P = 128
B = 2
T = 512
TT = T // P
E = 8
FF = 512
FC = FF // P
S = 32
SE = 64
SH = 128
UE = B * FC
UP = 2 * UE
GP = 2 * B
PAIRS = E // 2
LEAD = 3
NZ = 4
NO = 4
NR = 2
NT = 2
SPLIT_AT = 4
WARM_UP = 8
LOGITS_AT = 3
EXP_AT = 4
COMBINE_T_AT = 8
SINES_AT = 9
FIRST_WEIGH_AT = 12
WEIGH_AT = 2

LN_EPS = 1e-5
TIME_EPS = 1e-8
GAMMA_EPS = 1e-8
ROUND = 1.5 * 2.0 ** 23
PI_BELOW = 3.1415925
TWO_PI_HIGH = 6.28125
TWO_PI_LOW = 2 * math.pi - TWO_PI_HIGH


PACK = {}
for _name, _rows, _cols in (
        ("subj_emb", S, SE), ("hyp_w1", SE, SH), ("hyp_b1", SH, 1), ("hyp_b2", SH, 1), ("ln_g", P, 1), ("ln_b", P, 1),
        ("sty_b1", SH // 2, 1), ("sty_b2", P, 2), ("router_w", P, E), ("exp_b1", P, E * FC), ("exp_b2", P, E),
        ("hyp_w2", SH, SH), ("sty_w1", SH, SH // 2), ("sty_w2", SH // 2, 2 * P)):
    _start = max((s + c for _, s, c in PACK.values()), default=0)
    PACK[_name] = (_rows, _start, _cols)
PACK_FIRST = PACK["hyp_w2"][1]
PACK_COLS = max(s + c for _, s, c in PACK.values())


def conditioned_experts_kernel(nc, x_tokens, x_features, subject_ids, theta, phi, params, exp_w, out):
    ctx = ExitStack()
    with ctx:
        def sb(name, shape, dtype=F32):
            return ctx.enter_context(nc.sbuf_tensor(name, shape, dtype))

        def sem(name):
            return ctx.enter_context(nc.semaphore(name))

        x_tok = sb("x_tok", [P, B * TT, P])
        xn_tok = sb("xn_tok", [P, B * TT, P])
        w_raw = sb("w_raw", [P, E, 2 * FF])
        w_hi = [sb(f"w_hi{i}", [P, 2 * FF], F32R) for i in range(2)]
        w_lo = [sb(f"w_lo{i}", [P, 2 * FF], F32R) for i in range(2)]
        b1_now = [sb(f"b1_now{i}", [P, FC]) for i in range(2)]
        h_all = sb("h_all", [P, B, T])
        h_hi = sb("h_hi", [P, B, T], F32R)
        h_lo = sb("h_lo", [P, B, T], F32R)
        hid = [sb(f"hid{i}", [P, T]) for i in range(NR)]
        hid_hi = [sb(f"hid_hi{i}", [P, T], F32R) for i in range(NZ)]
        hid_lo = [sb(f"hid_lo{i}", [P, T], F32R) for i in range(NZ)]
        weighted = [sb(f"weighted{i}", [P, T]) for i in range(NT)]
        y_sum = sb("y_sum", [P, B, T])
        combine_all = sb("combine_all", [P, E, B * T])
        out_tok = sb("out_tok", [P, B, T])

        packed = sb("packed", [P, PACK_COLS])

        def param(name):
            rows, start, cols = PACK[name]
            return packed[0:rows, start:start + cols]

        b1_cols = param("exp_b1")
        b2_cols = param("exp_b2")
        ln_g, ln_b = param("ln_g"), param("ln_b")
        ids = sb("ids", [S, B], I32)
        ids_f = sb("ids_f", [S, B])
        onehot = sb("onehot", [S, B])
        emb_t = sb("emb_t", [SE, B])
        hyp_1 = sb("hyp_1", [SH, B])
        hyp_2 = sb("hyp_2", [SH, B])
        sty_1 = sb("sty_1", [SH // 2, B])
        gamma = sb("gamma", [P, B])
        beta = sb("beta", [P, B])
        soft = sb("soft", [P, 4 * B])

        stats = sb("stats", [P, B * TT, 6])
        mean_var = sb("mean_var", [P, B * TT, 2])
        tok_s = sb("tok_s", [P, B, 8, TT])
        VAR, LN, SEED, SQUARE, HALF_VAR, SQUARE_VAR, RSTD, SHIFT = range(8)
        t_stats = sb("t_stats", [P, B, 6])
        t_mv = sb("t_mv", [P, B, 2])
        t_s = sb("t_s", [P, B, 11])
        SHIFTED, SCALE, BIAS, MEAN = 7, 8, 9, 10
        g_squared = sb("g_squared", [P, 1])

        part = sb("part", [P, 2], I32)
        part_f = sb("part_f", [P, 4])
        part_odd = sb("part_odd", [P, 1], I32)
        rank_i = sb("rank_i", [P, B * TT, E], I32)
        rank = sb("rank", [P, B * TT, E])
        ident = sb("ident", [P, P])
        above = sb("above", [P, P])
        below = sb("below", [P, P])
        angles = sb("angles", [P, 2, B])
        ang = sb("ang", [P, 12, B])
        rot = sb("rot", [P, B, P])
        rot_t = sb("rot_t", [P, 3, B, P])

        r3 = [P, B * TT, E]
        shifted = sb("shifted", r3)
        e_prob = sb("e_prob", r3)
        prob = sb("prob", r3)
        pick = sb("pick", r3)
        mask1 = sb("mask1", r3)
        rest = sb("rest", r3)
        mask2 = sb("mask2", r3)
        gates = sb("gates", r3)
        combine = sb("combine", r3)
        red = sb("red", [P, 10, B * TT])
        combine_t = sb("combine_t", [E, B * T])
        combine_dram = nc.dram_tensor("combine_dram", (E, B * T), F32, kind="Internal").ap()

        z_ps = [ctx.enter_context(nc.psum_tensor(f"z_ps{i}", [P, T], F32)) for i in range(NZ)]
        o_ps = [ctx.enter_context(nc.psum_tensor(f"o_ps{i}", [P, T], F32)) for i in range(NO)]
        xn_t = [o_ps[0], o_ps[1]]
        small_ps = z_ps[2]
        logits_ps = o_ps[2]
        combine_ps = [o_ps[2], o_ps[3]]
        final_ps = [o_ps[0], z_ps[0]]
        final_rest_ps = [o_ps[1], z_ps[1]]

        x_loaded = [sem(f"x_loaded{b}") for b in range(B)]
        subject_loaded = sem("subject_loaded")
        params_loaded = sem("params_loaded")
        params2_loaded = sem("params2_loaded")
        y_init = sem("y_init")
        angles_loaded = sem("angles_loaded")
        w_first_loaded = sem("w_first_loaded")
        w_second_loaded = sem("w_second_loaded")
        w_rest_loaded = sem("w_rest_loaded")
        combine_stored = sem("combine_stored")
        cb_first_loaded = sem("cb_first_loaded")
        cb_second_loaded = sem("cb_second_loaded")
        cb_rest_loaded = sem("cb_rest_loaded")
        out_stored = sem("out_stored")
        consts_ready = sem("consts_ready")
        onehot_step = sem("onehot_step")
        subject_mm = sem("subject_mm")
        subject_act = sem("subject_act")
        soft_step = sem("soft_step")
        style_ready = sem("style_ready")
        tok_var = sem("tok_var")
        tok_seed = sem("tok_seed")
        tok_rstd = sem("tok_rstd")
        xn_by_dve = sem("xn_by_dve")
        xn_by_act = sem("xn_by_act")
        xn_t_ready = sem("xn_t_ready")
        t_var = sem("t_var")
        t_seed = sem("t_seed")
        affine_ready = sem("affine_ready")
        h_ready = sem("h_ready")
        h_hi_ready = sem("h_hi_ready")
        h_lo_ready = sem("h_lo_ready")
        logits_ready = sem("logits_ready")
        shifted_ready = sem("shifted_ready")
        e_prob_ready = sem("e_prob_ready")
        combine_ready = sem("combine_ready")
        combine_t_ps = sem("combine_t_ps")
        combine_t_ready = sem("combine_t_ready")
        angles_ready = sem("angles_ready")
        sines_ready = sem("sines_ready")
        masks_ready = sem("masks_ready")
        pool_step = sem("pool_step")
        rot_ready = sem("rot_ready")
        dve_step = sem("dve_step")
        w_hi_ready = sem("w_hi_ready")
        w_lo_ready = sem("w_lo_ready")
        z_ready = sem("z_ready")
        hid_ready = sem("hid_ready")
        hi_by_act = sem("hi_by_act")
        hi_by_dve = sem("hi_by_dve")
        lo_ready = sem("lo_ready")
        unit_done = sem("unit_done")
        weighted_ready = sem("weighted_ready")
        y_added = sem("y_added")
        final_ready = sem("final_ready")
        out_by_act = sem("out_by_act")
        out_by_dve = sem("out_by_dve")
        b1_copied = sem("b1_copied")

        block = ctx.enter_context(nc.Block())
        HALF = T // 2

        @block.sync
        def _(sp):
            def load_x(b):
                sp.dma_start(x_tok[:, b * TT:(b + 1) * TT, :], x_tokens[:, b]).then_inc(x_loaded[b], 16)

            def load_w(e, loaded):
                sp.dma_start(w_raw[:, e, :], exp_w[e]).then_inc(loaded, 16)

            load_x(0)
            sp.dma_start(ids[:, :], subject_ids.rearrange("(o b) -> o b", o=1).to_broadcast([S, B]))\
                .then_inc(subject_loaded, 16)
            sp.dma_start(packed[:, 0:PACK_FIRST], params[:, 0:PACK_FIRST]).then_inc(params_loaded, 16)
            load_x(1)
            sp.dma_start(packed[:, PACK_FIRST:], params[:, PACK_FIRST:]).then_inc(params2_loaded, 16)
            load_w(0, w_first_loaded)
            load_w(1, w_second_loaded)
            sp.dma_start(y_sum[:, :, :], x_features).then_inc(y_init, 16)
            for e in range(2, E):
                load_w(e, w_rest_loaded)
            sp.wait_ge(combine_t_ready, B)
            sp.dma_start(combine_dram, combine_t[:, :]).then_inc(combine_stored, 16)
            sp.wait_ge(combine_stored, 16)
            for e in range(E):
                loaded = cb_first_loaded if e == 0 else cb_second_loaded if e == 1 else cb_rest_loaded
                sp.dma_start(combine_all[:, e, :],
                             combine_dram[e:e + 1, :].to_broadcast([P, B * T])).then_inc(loaded, 16)
            for b in range(B):
                sp.wait_ge(out_by_act, b + 1)
                sp.dma_start(out[:, b, 0:HALF], out_tok[:, b, 0:HALF]).then_inc(out_stored, 16)
            sp.wait_ge(out_stored, 2 * B * 16)

        @block.gpsimd
        def _(pool):
            nc.gpsimd.iota(part[:, 0:1], [[0, 1]], base=0, channel_multiplier=1).then_inc(consts_ready, 1)
            nc.gpsimd.memset(ident[:, :], 0.0).then_inc(consts_ready, 1)
            pool.wait_ge(consts_ready, 2)
            nc.gpsimd.affine_select(out=ident[:, :], in_=ident[:, :], compare_op=ALU.not_equal, fill=1.0,
                                    base=0, pattern=[[-1, P]], channel_multiplier=1).then_inc(consts_ready, 1)
            nc.gpsimd.tensor_copy(part_f[:, 0:1], part[:, 0:1]).then_inc(consts_ready, 1)
            pool.wait_ge(subject_loaded, 16)
            nc.gpsimd.tensor_scalar(ids_f[:, :], ids[:, :], float(S - 1), 0.0, ALU.min, ALU.max)\
                .then_inc(onehot_step, 1)
            pool.wait_ge(onehot_step, 1)
            pool.wait_ge(consts_ready, 4)
            nc.gpsimd.tensor_scalar(onehot[:, :], ids_f[:, :], part_f[0:S, 0:1], None, ALU.is_equal)\
                .then_inc(onehot_step, 1)
            for n, a in enumerate((theta, phi)):
                pool.dma_start(angles[:, n, :], a.rearrange("(o b) -> o b", o=1).to_broadcast([P, B]))\
                    .then_inc(angles_loaded, 16)
            nc.gpsimd.iota(rank_i[:, :, :], [[0, B * TT], [-1, E]], base=E, channel_multiplier=0)\
                .then_inc(consts_ready, 1)
            for m in (above, below):
                nc.gpsimd.memset(m[:, :], 0.0).then_inc(consts_ready, 1)
            for n, (m, base) in enumerate(((above, 1), (below, -1))):
                pool.wait_ge(consts_ready, 6 + n)
                nc.gpsimd.affine_select(out=m[:, :], in_=m[:, :], compare_op=ALU.not_equal, fill=1.0,
                                        base=base, pattern=[[-1, P]], channel_multiplier=1)\
                    .then_inc(consts_ready, 1)

            def split_low(i, k, half):
                cols = slice(half * FF, (half + 1) * FF)
                pool.wait_ge(w_hi_ready, 4 * i + 2 * k + half + 1)
                nc.gpsimd.tensor_tensor(w_lo[k % 2][:, cols], w_raw[:, 2 * i + k, cols],
                                        w_hi[k % 2][:, cols].bitcast(F32), ALU.subtract)\
                    .then_inc(w_lo_ready, 1)

            done = [0]

            def settle(ins):
                done[0] += 1
                ins.then_inc(pool_step, 1)
                pool.wait_ge(pool_step, done[0])

            def sine_arguments():
                tt, ts = nc.gpsimd.tensor_tensor, nc.gpsimd.tensor_scalar
                pool.wait_ge(angles_loaded, 32)
                pool.wait_ge(masks_ready, 2)
                settle(ts(ang[:, 0, :], angles[:, 0, :], part_f[:, 2:3], None, ALU.mult))
                settle(ts(ang[:, 1, :], angles[:, 1, :], part_f[:, 1:2], None, ALU.mult))
                settle(tt(ang[:, 2, :], ang[:, 0, :], ang[:, 1, :], ALU.add))
                settle(ts(ang[:, 3, :], ang[:, 2, :], 1 / (2 * math.pi), ROUND, ALU.mult, ALU.add))
                settle(ts(ang[:, 4, :], ang[:, 3, :], -ROUND, None, ALU.add))
                settle(ts(ang[:, 5, :], ang[:, 4, :], -TWO_PI_HIGH, None, ALU.mult))
                settle(tt(ang[:, 6, :], ang[:, 2, :], ang[:, 5, :], ALU.add))
                settle(ts(ang[:, 5, :], ang[:, 4, :], -TWO_PI_LOW, None, ALU.mult))
                settle(tt(ang[:, 7, :], ang[:, 6, :], ang[:, 5, :], ALU.add))
                settle(ts(ang[:, 8, :], ang[:, 7, :], PI_BELOW, -PI_BELOW, ALU.min, ALU.max))
                settle(ts(ang[:, 7, :], ang[:, 8, :], 0.0, 2.0, ALU.max, ALU.mult))
                settle(tt(ang[:, 6, :], ang[:, 7, :], ang[:, 8, :], ALU.subtract))
                ts(ang[:, 9, :], ang[:, 6, :], -1.0, math.pi / 2, ALU.mult, ALU.add).then_inc(angles_ready, 1)

            def rotations():
                tt, ts = nc.gpsimd.tensor_tensor, nc.gpsimd.tensor_scalar
                pool.wait_ge(sines_ready, 2)
                settle(ts(ang[:, 0, :], ang[:, 10, :], part_f[:, 3:4], None, ALU.mult))
                settle(tt(ang[:, 1, :], ang[:, 0, :], ang[:, 10, :], ALU.subtract))
                for b in range(B):
                    for n, (m, c) in enumerate(((ident, 11), (below, 0), (above, 1))):
                        settle(ts(rot_t[:, n, b, :], m[:, :], ang[:, c, b:b + 1], None, ALU.mult))
                for b in range(B):
                    settle(tt(rot_t[:, 0, b, :], rot_t[:, 0, b, :], rot_t[:, 1, b, :], ALU.add))
                for b in range(B):
                    tt(rot[:, b, :], rot_t[:, 0, b, :], rot_t[:, 2, b, :], ALU.add).then_inc(rot_ready, 1)

            def add_group(i, q, first=False):
                pool.wait_ge(weighted_ready, GP * i + q + 1)
                b = q % B
                if first:
                    pool.wait_ge(y_init, 16)
                else:
                    pool.wait_ge(y_added, GP * i + q - B + 1)
                nc.gpsimd.tensor_tensor(y_sum[:, b, :], y_sum[:, b, :], weighted[q % NT][:, :], ALU.add)\
                    .then_inc(y_added, 1)

            def pair(i, first=False, last=False):
                if not first:
                    add_group(i, -1)
                split_low(i, 1, 0)
                split_low(i, 1, 1)
                if first:
                    rotations()
                else:
                    add_group(i, 0)
                    add_group(i, 1)
                if not last:
                    split_low(i, 2, 0)
                    split_low(i, 2, 1)
                    if first:
                        add_group(i, 0, first)
                        add_group(i, 1, first)
                    add_group(i, 2)

            pool.wait_ge(w_first_loaded, 16)
            for half in range(2):
                cols = slice(half * FF, (half + 1) * FF)
                nc.gpsimd.tensor_copy(w_hi[0][:, cols], w_raw[:, 0, cols]).then_inc(w_hi_ready, 1)
                split_low(0, 0, half)
            sine_arguments()
            pair(0, first=True)
            with pool.Fori(1, PAIRS - 1) as i:
                pair(i)
            pair(PAIRS - 1, last=True)

        @block.scalar
        def _(act):
            nc.scalar.preload_act_table_set("natural_log_exp_and_others")
            def seed(b):
                act.wait_ge(tok_var, b + 1)
                nc.scalar.activation(tok_s[:, b, LN, :], tok_s[:, b, VAR, :], ACT.Ln).then_inc(tok_seed, 1)
                act.wait_ge(tok_seed, 2 * b + 1)
                nc.scalar.activation(tok_s[:, b, SEED, :], tok_s[:, b, LN, :], ACT.Exp, scale=-0.5)\
                    .then_inc(tok_seed, 1)

            def normalise_half(b):
                act.wait_ge(tok_rstd, 2 * (b + 1))
                for t in range(TT // 2, TT):
                    nc.scalar.activation(xn_tok[:, b * TT + t, :], x_tok[:, b * TT + t, :], ACT.Identity,
                                         scale=tok_s[:, b, RSTD, t:t + 1], bias=tok_s[:, b, SHIFT, t:t + 1])\
                        .then_inc(xn_by_act, 1)

            def time_seed(b):
                act.wait_ge(t_var, b + 1)
                nc.scalar.activation(t_s[:, b, LN:LN + 1], t_s[:, b, VAR:VAR + 1], ACT.Ln).then_inc(t_seed, 1)
                act.wait_ge(t_seed, 2 * b + 1)
                nc.scalar.activation(t_s[:, b, SEED:SEED + 1], t_s[:, b, LN:LN + 1], ACT.Exp, scale=-0.5)\
                    .then_inc(t_seed, 1)

            def h_float(b):
                act.wait_ge(affine_ready, 2 * (b + 1))
                nc.scalar.activation(h_hi[:, b, :], xn_t[b][:, :], ACT.Identity,
                                     scale=t_s[:, b, SCALE:SCALE + 1], bias=t_s[:, b, BIAS:BIAS + 1])\
                    .then_inc(h_hi_ready, 1)
                nc.scalar.activation(h_all[:, b, :], xn_t[b][:, :], ACT.Identity,
                                     scale=t_s[:, b, SCALE:SCALE + 1], bias=t_s[:, b, BIAS:BIAS + 1])\
                    .then_inc(h_ready, 1)

            act.wait_ge(subject_mm, 1)
            nc.scalar.copy(emb_t[:, :], small_ps[0:SE, 0:B]).then_inc(subject_act, 1)
            act.wait_ge(subject_mm, 2)
            nc.scalar.activation(hyp_1[:, :], small_ps[:, 2:2 + B], ACT.Relu, bias=param("hyp_b1"))\
                .then_inc(subject_act, 1)
            seed(0)
            act.wait_ge(subject_mm, 3)
            nc.scalar.activation(hyp_2[:, :], small_ps[:, 4:4 + B], ACT.Identity, bias=param("hyp_b2"))\
                .then_inc(subject_act, 1)
            normalise_half(0)
            act.wait_ge(subject_mm, 4)
            nc.scalar.activation(sty_1[:, :], small_ps[0:SH // 2, 6:6 + B], ACT.Relu, bias=param("sty_b1"))\
                .then_inc(subject_act, 1)
            seed(1)
            act.wait_ge(subject_mm, 5)
            graw, braw = small_ps[:, 8:8 + B], small_ps[:, 10:10 + B]
            gamma_b, beta_b = param("sty_b2")[:, 0:1], param("sty_b2")[:, 1:2]
            nc.scalar.activation(soft[:, 0:B], graw, ACT.Abs, bias=gamma_b).then_inc(soft_step, 1)
            nc.scalar.activation(soft[:, 3 * B:4 * B], graw, ACT.Relu, bias=gamma_b).then_inc(soft_step, 1)
            act.wait_ge(soft_step, 1)
            nc.scalar.activation(soft[:, B:2 * B], soft[:, 0:B], ACT.Exp, scale=-1.0).then_inc(soft_step, 1)
            nc.scalar.activation(beta[:, :], braw, ACT.Identity, bias=beta_b).then_inc(soft_step, 1)
            act.wait_ge(soft_step, 3)
            nc.scalar.activation(soft[:, 2 * B:3 * B], soft[:, B:2 * B], ACT.Ln, bias=1.0).then_inc(soft_step, 1)

            def copy_b1(i, k):
                nc.scalar.copy(b1_now[k % 2][:, :], b1_cols[:, bass.ds((2 * i + k) * FC, FC)])\
                    .then_inc(b1_copied, 1)

            def split_high(i, k, half):
                cols = slice(half * FF, (half + 1) * FF)
                nc.scalar.activation(w_hi[k % 2][:, cols], w_raw[:, 2 * i + k, cols], ACT.Copy)\
                    .then_inc(w_hi_ready, 1)

            def hidden(i, k, first):
                u = UP * i + k
                bias = b1_now[k // UE][:, k % FC:k % FC + 1]
                act.wait_ge(z_ready, u + 1)
                if k % 2 == 0:
                    if not (first and k < NZ):
                        act.wait_ge(unit_done, u - NZ + 1)
                    nc.scalar.activation(hid_hi[k % NZ][:, :], z_ps[k % NZ][:, :], ACT.Relu, bias=bias)\
                        .then_inc(hi_by_act, 1)
                if not (first and k < NR):
                    act.wait_ge(lo_ready, u - NR + 1)
                nc.scalar.activation(hid[k % NR][:, :], z_ps[k % NZ][:, :], ACT.Relu, bias=bias)\
                    .then_inc(hid_ready, 1)

            time_seed(0)
            normalise_half(1)
            h_float(0)
            copy_b1(0, 0)
            time_seed(1)

            def exponentials():
                act.wait_ge(shifted_ready, 1)
                nc.scalar.activation(e_prob[:, :, :], shifted[:, :, :], ACT.Exp).then_inc(e_prob_ready, 1)

            def combine_columns():
                for b in range(B):
                    act.wait_ge(combine_t_ps, b + 1)
                    nc.scalar.copy(combine_t[:, b * T:(b + 1) * T], combine_ps[b][0:E, :])\
                        .then_inc(combine_t_ready, 1)

            def sines():
                act.wait_ge(angles_ready, 1)
                nc.scalar.activation(ang[:, 10, :], ang[:, 8, :], ACT.Sin).then_inc(sines_ready, 1)
                nc.scalar.activation(ang[:, 11, :], ang[:, 9, :], ACT.Sin).then_inc(sines_ready, 1)

            extra = {EXP_AT: exponentials, COMBINE_T_AT: combine_columns, SINES_AT: sines}

            def pair(i, first=False, last=False):
                for k in range(UP):
                    if k % UE == 0:
                        act.wait_ge(b1_copied, 2 * i + k // UE + 1)
                    hidden(i, k, first)
                    if first and k == 0:
                        h_float(1)
                    if first and k in extra:
                        extra[k]()
                    half = k % UE - SPLIT_AT
                    if half in (0, 1) and not (last and k >= UE):
                        if first and half == 0:
                            if k < UE:
                                act.wait_ge(w_second_loaded, 16)
                            else:
                                act.wait_ge(w_rest_loaded, (E - 2) * 16)
                        if half == 0:
                            copy_b1(i, k // UE + 1)
                        split_high(i, k // UE + 1, half)

            pair(0, first=True)
            with act.Fori(1, PAIRS - 1) as i:
                pair(i)
            pair(PAIRS - 1, last=True)
            for b in range(B):
                act.wait_ge(final_ready, 2 * b + 1)
                nc.scalar.copy(out_tok[:, b, 0:HALF], final_ps[b][:, 0:HALF]).then_inc(out_by_act, 1)
            for b in range(B):
                act.wait_ge(out_by_dve, b + 1)
                act.dma_start(out[:, b, HALF:T], out_tok[:, b, HALF:T]).then_inc(out_stored, 16)

        @block.vector
        def _(dve):
            done = [0]

            def step(ins):
                done[0] += 1
                ins.then_inc(dve_step, 1)
                return done[0]

            def settle(ins):
                dve.wait_ge(dve_step, step(ins))

            def token_stats(b):
                dve.wait_ge(x_loaded[b], 16)
                for t in range(TT):
                    n = step(nc.vector.bn_stats(stats[:, b * TT + t, :], x_tok[:, b * TT + t, :]))
                return n - TT

            def token_variances(b, n):
                s = tok_s[:, b]
                for t in range(TT):
                    dve.wait_ge(dve_step, n + 1 + t)
                    m = step(nc.vector.bn_aggr(mean_var[:, b * TT + t, :], stats[:, b * TT + t, :]))
                dve.wait_ge(dve_step, m)
                var = mean_var[:, b * TT:(b + 1) * TT, 1]
                nc.vector.tensor_scalar(s[:, VAR, :], var, LN_EPS, None, ALU.add).then_inc(tok_var, 1)
                dve.wait_ge(tok_var, b + 1)
                step(nc.vector.tensor_scalar(s[:, HALF_VAR, :], s[:, VAR, :], -0.5, None, ALU.mult))

            def token_rstd(b):
                s = tok_s[:, b]
                dve.wait_ge(tok_seed, 2 * (b + 1))
                settle(nc.vector.tensor_tensor(s[:, SQUARE, :], s[:, SEED, :], s[:, SEED, :], ALU.mult))
                settle(nc.vector.tensor_tensor(s[:, SQUARE_VAR, :], s[:, SQUARE, :], s[:, HALF_VAR, :], ALU.mult))
                nc.vector.scalar_tensor_tensor(s[:, RSTD, :], s[:, SQUARE_VAR, :], 1.5, s[:, SEED, :],
                                               ALU.add, ALU.mult).then_inc(tok_rstd, 1)
                dve.wait_ge(tok_rstd, 2 * b + 1)
                nc.vector.scalar_tensor_tensor(s[:, SHIFT, :], mean_var[:, b * TT:(b + 1) * TT, 0], -1.0,
                                               s[:, RSTD, :], ALU.mult, ALU.mult).then_inc(tok_rstd, 1)

            def normalise_half(b):
                for t in range(TT // 2):
                    nc.vector.tensor_scalar(xn_tok[:, b * TT + t, :], x_tok[:, b * TT + t, :],
                                            mean_var[:, b * TT + t, 0:1], tok_s[:, b, RSTD, t:t + 1],
                                            ALU.subtract, ALU.mult).then_inc(xn_by_dve, 1)

            def time_stats(b):
                s = t_s[:, b]
                dve.wait_ge(xn_t_ready, b + 1)
                settle(nc.vector.bn_stats(t_stats[:, b, :], xn_t[b][:, :]))
                settle(nc.vector.bn_aggr(t_mv[:, b, :], t_stats[:, b, :]))
                nc.vector.tensor_scalar(s[:, VAR:VAR + 1], t_mv[:, b, 1:2], g_squared[:, :], TIME_EPS,
                                        ALU.mult, ALU.add).then_inc(t_var, 1)
                n = step(nc.vector.tensor_scalar(s[:, SQUARE:SQUARE + 1], t_mv[:, b, 0:1], ln_g, ln_b,
                                                 ALU.mult, ALU.add))
                dve.wait_ge(t_var, b + 1)
                step(nc.vector.tensor_scalar(s[:, HALF_VAR:HALF_VAR + 1], s[:, VAR:VAR + 1], -0.5, None,
                                             ALU.mult))
                dve.wait_ge(dve_step, n)
                settle(nc.vector.tensor_scalar(s[:, MEAN:MEAN + 1], s[:, SQUARE:SQUARE + 1], ln_b, -1.0,
                                               ALU.subtract, ALU.mult))

            def affine(b):
                s = t_s[:, b]

                def col(n):
                    return s[:, n:n + 1]
                dve.wait_ge(t_seed, 2 * (b + 1))
                settle(nc.vector.tensor_scalar(col(SQUARE_VAR), col(SEED), col(SEED), col(HALF_VAR),
                                               ALU.mult, ALU.mult))
                settle(nc.vector.tensor_scalar(col(RSTD), col(SQUARE_VAR), 1.5, col(SEED), ALU.add, ALU.mult))
                n = step(nc.vector.tensor_scalar(col(SHIFTED), col(MEAN), col(RSTD), None, ALU.mult))
                nc.vector.tensor_scalar(col(SCALE), col(RSTD), ln_g, gamma[:, b:b + 1], ALU.mult, ALU.mult)\
                    .then_inc(affine_ready, 1)
                dve.wait_ge(dve_step, n)
                nc.vector.tensor_scalar(col(BIAS), col(SHIFTED), gamma[:, b:b + 1], beta[:, b:b + 1],
                                        ALU.mult, ALU.add).then_inc(affine_ready, 1)

            def feature_masks():
                dve.wait_ge(consts_ready, 4)
                step(nc.vector.tensor_scalar(part[:, 1:2], part[:, 0:1], 2, None, ALU.bitwise_and))
                n = step(nc.vector.tensor_scalar(part_odd[:, :], part[:, 0:1], 1, None, ALU.bitwise_and))
                dve.wait_ge(dve_step, n)
                n = step(nc.vector.tensor_scalar(part_f[:, 1:2], part[:, 1:2], 0.5, None, ALU.mult))
                nc.vector.tensor_copy(part_f[:, 3:4], part_odd[:, :]).then_inc(masks_ready, 1)
                dve.wait_ge(dve_step, n)
                nc.vector.tensor_scalar(part_f[:, 2:3], part_f[:, 1:2], -1.0, 1.0, ALU.mult, ALU.add)\
                    .then_inc(masks_ready, 1)

            def split_h(b):
                dve.wait_ge(h_ready, b + 1)
                nc.vector.tensor_tensor(h_lo[:, b, :], h_all[:, b, :], h_hi[:, b, :].bitcast(F32), ALU.subtract)\
                    .then_inc(h_lo_ready, 1)

            n = token_stats(0)
            token_variances(0, n)
            n = token_stats(1)
            token_rstd(0)
            normalise_half(0)
            token_variances(1, n)
            dve.wait_ge(params_loaded, 16)
            settle(nc.vector.tensor_tensor(g_squared[:, :], ln_g, ln_g, ALU.mult))
            time_stats(0)
            token_rstd(1)
            dve.wait_ge(soft_step, 5)
            settle(nc.vector.scalar_tensor_tensor(gamma[:, :], soft[:, 2 * B:3 * B], GAMMA_EPS,
                                                  soft[:, 3 * B:4 * B], ALU.add, ALU.add))
            affine(0)
            normalise_half(1)
            split_h(0)
            time_stats(1)
            affine(1)
            feature_masks()

            def over(m):
                return red[:, m, :].unsqueeze(2).to_broadcast([P, B * TT, E])

            def reduce(m, src, op):
                settle(nc.vector.tensor_reduce(red[:, m, :], src[:, :, :], axis=AX_X, op=op))

            def tt(o, a, b_, op):
                settle(nc.vector.tensor_tensor(o[:, :, :], a[:, :, :], b_, op))

            def first_at(m, src, mask):
                reduce(m, src, ALU.max)
                tt(pick, src, over(m), ALU.is_equal)
                tt(pick, pick, rank[:, :, :], ALU.mult)
                reduce(m + 1, pick, ALU.max)
                tt(mask, rank, over(m + 1), ALU.is_equal)

            def route_a():
                dve.wait_ge(consts_ready, 5)
                settle(nc.vector.tensor_copy(rank[:, :, :], rank_i[:, :, :]))
                dve.wait_ge(logits_ready, B)
                settle(nc.vector.tensor_reduce(red[:, 0, :], logits_ps[:, 0:B * TT * E].rearrange("p (j e) -> p j e", e=E), axis=AX_X, op=ALU.max))
                nc.vector.tensor_tensor(shifted[:, :, :], logits_ps[:, 0:B * TT * E].rearrange("p (j e) -> p j e", e=E), over(0), ALU.subtract)\
                    .then_inc(shifted_ready, 1)

            def route_b():
                dve.wait_ge(e_prob_ready, 1)
                reduce(1, e_prob, ALU.add)
                settle(nc.vector.reciprocal(red[:, 2, :], red[:, 1, :]))
                tt(prob, e_prob, over(2), ALU.mult)
                first_at(3, prob, mask1)

            def route_c():
                settle(nc.vector.scalar_tensor_tensor(rest[:, :, :], mask1[:, :, :], -2.0, prob[:, :, :],
                                                      ALU.mult, ALU.add))
                first_at(5, rest, mask2)
                tt(mask1, mask1, mask2[:, :, :], ALU.add)
                tt(gates, prob, mask1[:, :, :], ALU.mult)
                reduce(7, gates, ALU.add)
                settle(nc.vector.reciprocal(red[:, 8, :], red[:, 7, :]))
                nc.vector.tensor_tensor(combine[:, :, :], gates[:, :, :], over(8), ALU.mult)\
                    .then_inc(combine_ready, 1)

            extra = {LOGITS_AT: route_a, EXP_AT: route_b, EXP_AT + 1: route_c}

            def split_unit(i, k, first):
                dve.wait_ge(hid_ready, UP * i + k + 1)
                if not (first and k < NZ):
                    dve.wait_ge(unit_done, UP * i + k - NZ + 1)
                if k % 2 == 1:
                    nc.vector.tensor_copy(hid_hi[k % NZ][:, :], hid[k % NR][:, :]).then_inc(hi_by_dve, 1)
                    dve.wait_ge(hi_by_dve, UP // 2 * i + (k + 1) // 2)
                nc.vector.tensor_tensor(hid_lo[k % NZ][:, :], hid[k % NR][:, :],
                                        hid_hi[k % NZ][:, :].bitcast(F32), ALU.subtract).then_inc(lo_ready, 1)

            def weigh_group(i, q, first=False):
                b, e = q % B, 2 * i + q // B
                dve.wait_ge(unit_done, UP * i + (q + 1) * FC)
                if not (first and q < NT):
                    dve.wait_ge(y_added, GP * i + q - NT + 1)
                nc.vector.scalar_tensor_tensor(weighted[q % NT][:, :], o_ps[q % NO][:, :],
                                               b2_cols[:, bass.ds(e, 1)],
                                               combine_all[:, e, b * T:(b + 1) * T], ALU.add, ALU.mult)\
                    .then_inc(weighted_ready, 1)

            first_weighed = {FIRST_WEIGH_AT: 0, FIRST_WEIGH_AT + 1: 1, UP - FC + WEIGH_AT: 2}
            for k in range(UP):
                split_unit(0, k, first=True)
                if k == 0:
                    split_h(1)
                if k in extra:
                    extra[k]()
                if k in first_weighed:
                    q = first_weighed[k]
                    if q == 0:
                        dve.wait_ge(cb_first_loaded, 16)
                    if q == B:
                        dve.wait_ge(cb_second_loaded, 16)
                    weigh_group(0, q, first=True)
            dve.wait_ge(cb_rest_loaded, (E - 2) * 16)
            with dve.Fori(1, PAIRS) as i:
                for k in range(UP):
                    split_unit(i, k, first=False)
                    if k % FC == WEIGH_AT:
                        weigh_group(i, k // FC - 1)
            weigh_group(PAIRS, -1)
            for b in range(B):
                dve.wait_ge(final_ready, 2 * b + 2)
                nc.vector.tensor_copy(out_tok[:, b, HALF:T], final_rest_ps[b][:, 0:HALF]).then_inc(out_by_dve, 1)

        @block.tensor
        def _(pe):
            def mm(o, l, r, start=True, stop=True):
                return nc.tensor.matmul(o, l, r, start=start, stop=stop)

            def transposed(o, i, n=P):
                return nc.tensor.transpose(o, i, ident[0:n, 0:n])

            pe.wait_ge(onehot_step, 2)
            pe.wait_ge(params_loaded, 16)
            mm(small_ps[0:SE, 0:B], param("subj_emb"), onehot[:, :]).then_inc(subject_mm, 1)
            pe.wait_ge(subject_act, 1)
            mm(small_ps[:, 2:2 + B], param("hyp_w1"), emb_t[:, :]).then_inc(subject_mm, 1)
            pe.wait_ge(params2_loaded, 16)
            pe.wait_ge(subject_act, 2)
            mm(small_ps[:, 4:4 + B], param("hyp_w2"), hyp_1[:, :]).then_inc(subject_mm, 1)
            pe.wait_ge(subject_act, 3)
            mm(small_ps[0:SH // 2, 6:6 + B], param("sty_w1"), hyp_2[:, :]).then_inc(subject_mm, 1)

            def transpose_tokens(b):
                for t in range(TT):
                    if t < TT // 2:
                        pe.wait_ge(xn_by_dve, b * TT // 2 + t + 1)
                    else:
                        pe.wait_ge(xn_by_act, b * TT // 2 + t - TT // 2 + 1)
                    m = transposed(xn_t[b][:, t * P:(t + 1) * P], xn_tok[:, b * TT + t, :])
                m.then_inc(xn_t_ready, 1)

            pe.wait_ge(consts_ready, 3)
            transpose_tokens(0)
            pe.wait_ge(subject_act, 4)
            mm(small_ps[:, 8:8 + B], param("sty_w2")[:, 0:P], sty_1[:, :])
            mm(small_ps[:, 10:10 + B], param("sty_w2")[:, P:2 * P], sty_1[:, :]).then_inc(subject_mm, 1)

            def high_passes(i, k, first=False):
                parity, b, c = k // UE, k // FC % B, k % FC
                if k % UE == 0:
                    pe.wait_ge(w_lo_ready, 4 * i + 2 * parity + 1)
                if not (first and k < NZ):
                    pe.wait_ge(hid_ready, UP * i + k - NZ + 1)
                elif k == 2:
                    pe.wait_ge(soft_step, 5)
                if first and k in (0, FC):
                    pe.wait_ge(h_hi_ready, b + 1)
                z = z_ps[k % NZ][:, :]
                cols = slice(c * P, (c + 1) * P)
                mm(z, w_hi[parity][:, cols], h_hi[:, b, :], True, False)
                mm(z, w_lo[parity][:, cols], h_hi[:, b, :], False, False)

            def low_pass(k, first=False):
                parity, b, c = k // UE, k // FC % B, k % FC
                if first and k in (0, FC):
                    pe.wait_ge(h_lo_ready, b + 1)
                mm(z_ps[k % NZ][:, :], w_hi[parity][:, c * P:(c + 1) * P], h_lo[:, b, :], False, True)\
                    .then_inc(z_ready, 1)

            def second_product(i, k, first=False):
                parity, c = k // UE % 2, k % FC
                if k % UE == 0:
                    pe.wait_ge(w_lo_ready, 4 * i + 2 * parity + 2)
                if c == 0:
                    if not first:
                        pe.wait_ge(weighted_ready, GP * i + k // FC - NO + 1)
                    elif k >= 2 * FC:
                        pe.wait_ge(combine_t_ready, k // FC - 1)
                o = o_ps[k // FC % NO][:, :]
                cols = slice(FF + c * P, FF + (c + 1) * P)
                pe.wait_ge(hi_by_act if k % 2 == 0 else hi_by_dve, UP // 2 * i + k // 2 + 1)
                mm(o, w_hi[parity][:, cols], hid_hi[k % NZ][:, :], c == 0, False)
                mm(o, w_lo[parity][:, cols], hid_hi[k % NZ][:, :], False, False)
                pe.wait_ge(lo_ready, UP * i + k + 1)
                mm(o, w_hi[parity][:, cols], hid_lo[k % NZ][:, :], False, c == FC - 1).then_inc(unit_done, 1)

            def logits(b):
                if b == 0:
                    pe.wait_ge(params_loaded, 16)
                pe.wait_ge(h_ready, b + 1)
                for j in range(b * TT, (b + 1) * TT):
                    m = mm(logits_ps[:, j * E:(j + 1) * E], h_all[:, b, (j % TT) * P:(j % TT + 1) * P],
                           param("router_w"))
                m.then_inc(logits_ready, 1)

            def combine_transposes():
                pe.wait_ge(combine_ready, 1)
                for b in range(B):
                    for t in range(TT):
                        m = transposed(combine_ps[b][0:E, t * P:(t + 1) * P], combine[:, b * TT + t, :])
                    m.then_inc(combine_t_ps, 1)

            for n in range(WARM_UP):
                mm(z_ps[3][:, 0:P], ident[:, :], ident[:, :])
            transpose_tokens(1)
            for k in range(LEAD):
                high_passes(0, k, first=True)
            for k in range(LEAD):
                low_pass(k, first=True)
            for k in range(LEAD, UP):
                if k == FC:
                    logits(0)
                high_passes(0, k, first=True)
                low_pass(k, first=True)
                if k == FC:
                    logits(1)
                if k >= LEAD:
                    second_product(0, k - LEAD, first=True)
                if k == COMBINE_T_AT - 1:
                    combine_transposes()
            with pe.Fori(1, PAIRS) as i:
                for k in range(UP):
                    high_passes(i, k)
                    low_pass(k)
                    second_product(i, k - LEAD)
            for k in range(-LEAD, 0):
                second_product(PAIRS, k)

            pe.wait_ge(rot_ready, B)
            pe.wait_ge(weighted_ready, E * B - B)
            pe.wait_ge(hid_ready, E * UE)
            for b in range(B):
                halves = [(final_ps[b], slice(0, HALF)), (final_rest_ps[b], slice(HALF, T))]
                pe.wait_ge(y_added, E * B - 2 * B + b + 1)
                for bank, cols in halves:
                    mm(bank[:, 0:HALF], rot[:, b, :], y_sum[:, b, cols], True, False)
                pe.wait_ge(weighted_ready, E * B - B + b + 1)
                for bank, cols in halves:
                    mm(bank[:, 0:HALF], rot[:, b, :], weighted[b][:, cols], False, True).then_inc(final_ready, 1)


def kernel(**inputs):
    import numpy as np
    import concourse.bacc as bacc
    from concourse.bass_utils import run_bass_kernel_spmd

    own = {k.removeprefix("L0_cond_"): np.asarray(v) for k, v in inputs.items()}
    columns = {
        "subj_emb": own["subj_emb"], "hyp_w1": own["hyp_w1"], "hyp_w2": own["hyp_w2"],
        "sty_w1": own["sty_w1"], "sty_w2": own["sty_w2"], "router_w": own["router_w"],
        "hyp_b1": own["hyp_b1"][:, None], "hyp_b2": own["hyp_b2"][:, None], "sty_b1": own["sty_b1"][:, None],
        "ln_g": own["ln_g"][:, None], "ln_b": own["ln_b"][:, None],
        "sty_b2": own["sty_b2"].reshape(2, P).T,
        "exp_b1": own["exp_b1"].reshape(E * FC, P).T,
        "exp_b2": own["exp_b2"].T,
    }
    params = np.zeros((P, PACK_COLS), own["ln_g"].dtype)
    for name, (rows, start, cols) in PACK.items():
        params[0:rows, start:start + cols] = columns[name]
    w2_rows = own["exp_w2"].reshape(E, FC, P, P).transpose(0, 2, 1, 3).reshape(E, P, FF)
    arrays = {
        "x_tokens": own["x"].reshape(B, TT, P, P).transpose(2, 0, 1, 3),
        "x_features": own["x"].transpose(2, 0, 1),
        "subject_ids": own["itok_B_6_14"],
        "theta": own["condB_theta"],
        "phi": own["condB_phi"],
        "params": params,
        "exp_w": np.concatenate([own["exp_w1"], w2_rows], axis=2),
    }
    arrays = {f"{k}_dram": np.ascontiguousarray(v) for k, v in arrays.items()}

    nc = bacc.Bacc("TRN2", target_bir_lowering=False, num_devices=1)
    args = [nc.dram_tensor(k, v.shape, mybir.dt.from_np(v.dtype), kind="ExternalInput").ap()
            for k, v in arrays.items()]
    out = nc.dram_tensor("out_dram", (P, B, T), F32, kind="ExternalOutput").ap()
    conditioned_experts_kernel(nc, *args, out)
    got = run_bass_kernel_spmd(nc, [arrays], core_ids=[0]).results[0]["out_dram"]
    return np.ascontiguousarray(got.transpose(1, 2, 0))
```

```python
import math
from contextlib import ExitStack

import concourse.bass as bass
from concourse import mybir

ALU = mybir.AluOpType
ACT = mybir.ActivationFunctionType
AX_X = mybir.AxisListType.X
F32 = mybir.dt.float32
F32R = mybir.dt.float32r
I32 = mybir.dt.int32

P = 128
B = 2
T = 512
TT = T // P
E = 8
FF = 512
FC = FF // P
S = 32
SE = 64
SH = 128
UE = B * FC
UP = 2 * UE
GP = 2 * B
PAIRS = E // 2
GROUPS = E * B
LEAD = 3
NZ = 4
NO = 4
NR = 2
NT = 4
DT = 3
SPLIT_AT = 4
WARM_UP = 7
LOGITS_AT = 6
ROUTE_AT = 4
EXP_AT = 5
COMBINE_T_AT = 12
SINES_AT = 0
FIRST_WEIGHED = {15: 0, 16: 1, 18: 2, 20: 3}
ACT_HIGHS = (5, 7, 9, 11)
POOL_LOWS = (2, 4, 6, 8)
DVE_FROM = 6
WEIGH_AT = 2

LN_EPS = 1e-5
TIME_EPS = 1e-8
GAMMA_EPS = 1e-8
ROUND = 1.5 * 2.0 ** 23
PI_BELOW = 3.1415925
TWO_PI_HIGH = 6.28125
TWO_PI_LOW = 2 * math.pi - TWO_PI_HIGH


PACK = {}
for _name, _rows, _cols in (
        ("subj_emb", S, SE), ("hyp_w1", SE, SH), ("hyp_b1", SH, 1), ("hyp_b2", SH, 1), ("ln_g", P, 1), ("ln_b", P, 1),
        ("sty_b1", SH // 2, 1), ("sty_b2", P, 2), ("router_w", P, E), ("exp_b1", P, E * FC), ("exp_b2", P, E),
        ("hyp_w2", SH, SH), ("sty_w1", SH, SH // 2), ("sty_w2", SH // 2, 2 * P)):
    _start = max((s + c for _, s, c in PACK.values()), default=0)
    PACK[_name] = (_rows, _start, _cols)
PACK_FIRST = PACK["hyp_w2"][1]
PACK_COLS = max(s + c for _, s, c in PACK.values())


def unit_parts(k, first):
    if first:
        return k // FC % 2, k // UE, k % FC
    return k // UE, k // FC % B, k % FC


def highs_by_act(i, k, first):
    return UP // 2 * i + k // 2 + 1 + (sum(u <= k for u in ACT_HIGHS) if first else len(ACT_HIGHS))


def highs_by_dve(i, k, first):
    return UP // 2 * i + (k + 1) // 2 - (sum(u <= k for u in ACT_HIGHS) if first else len(ACT_HIGHS))


def lows_by_dve(i, k, first):
    return UP * i + k + 1 - (sum(u <= k for u in POOL_LOWS) if first else len(POOL_LOWS))


def conditioned_experts_kernel(nc, x_tokens, x_features, subject_ids, theta, phi, params, exp_w, out):
    ctx = ExitStack()
    with ctx:
        def sb(name, shape, dtype=F32):
            return ctx.enter_context(nc.sbuf_tensor(name, shape, dtype))

        def sem(name):
            return ctx.enter_context(nc.semaphore(name))

        x_tok = sb("x_tok", [P, B * TT, P])
        xn_tok = sb("xn_tok", [P, B * TT, P])
        w_raw = sb("w_raw", [P, E, 2 * FF])
        w_hi = [sb(f"w_hi{i}", [P, 2 * FF], F32R) for i in range(2)]
        w_lo = [sb(f"w_lo{i}", [P, 2 * FF], F32R) for i in range(2)]
        b1_now = [sb(f"b1_now{i}", [P, FC]) for i in range(2)]
        h_all = sb("h_all", [P, B, T])
        h_hi = sb("h_hi", [P, B, T], F32R)
        h_lo = sb("h_lo", [P, B, T], F32R)
        hid = [sb(f"hid{i}", [P, T]) for i in range(NR)]
        hid_hi = [sb(f"hid_hi{i}", [P, T], F32R) for i in range(NZ)]
        hid_lo = [sb(f"hid_lo{i}", [P, T], F32R) for i in range(NZ)]
        weighted = [sb(f"weighted{i}", [P, T]) for i in range(NT)]
        y_sum = sb("y_sum", [P, B, T])
        combine_all = sb("combine_all", [P, E, B * T])
        out_sb = sb("out_sb", [P, B, T])

        packed = sb("packed", [P, PACK_COLS])

        def param(name):
            rows, start, cols = PACK[name]
            return packed[0:rows, start:start + cols]

        b1_cols = param("exp_b1")
        b2_cols = param("exp_b2")
        ln_g, ln_b = param("ln_g"), param("ln_b")
        ids = sb("ids", [S, B], I32)
        onehot = sb("onehot", [S, 2, B])
        emb_t = sb("emb_t", [SE, B])
        hyp_1 = sb("hyp_1", [SH, B])
        hyp_2 = sb("hyp_2", [SH, B])
        sty_1 = sb("sty_1", [SH // 2, B])
        gamma = sb("gamma", [P, B])
        beta = sb("beta", [P, B])
        soft = sb("soft", [P, 4 * B])

        stats = sb("stats", [P, B * TT, 6])
        mean_var = sb("mean_var", [P, B * TT, 2])
        tok_s = sb("tok_s", [P, B, 7, TT])
        LN, SEED, SQUARE, HALF_VAR, SQUARE_VAR, RSTD, SHIFT = range(7)
        t_stats = sb("t_stats", [P, B, 6])
        t_mv = sb("t_mv", [P, B, 2])
        t_s = sb("t_s", [P, B, 12])
        SCALE, BIAS, MEAN, WIDTH, OFFSET = range(7, 12)
        g_squared = sb("g_squared", [P, 2])
        eps = sb("eps", [P, 2])

        part = sb("part", [P, 2], I32)
        part_f = sb("part_f", [P, 5])
        part_odd = sb("part_odd", [P, 1], I32)
        rank_i = sb("rank_i", [P, B * TT, E], I32)
        rank = sb("rank", [P, B * TT, E])
        ident = sb("ident", [P, P])
        above = sb("above", [P, P])
        below = sb("below", [P, P])
        angles = sb("angles", [P, 2, B])
        ang = sb("ang", [P, 12, B])
        rot = sb("rot", [P, B, P])
        rot_t = sb("rot_t", [P, 3, P])

        r3 = [P, B * TT, E]
        shifted = sb("shifted", r3)
        e_prob = sb("e_prob", r3)
        prob = sb("prob", r3)
        pick = sb("pick", r3)
        mask1 = sb("mask1", r3)
        rest = sb("rest", r3)
        mask2 = sb("mask2", r3)
        gates = sb("gates", r3)
        combine = sb("combine", [P, E, B * TT])
        red = sb("red", [P, 9, B * TT])
        combine_t = sb("combine_t", [E * B * TT, P])
        combine_dram = nc.dram_tensor("combine_dram", (E, B * T), F32, kind="Internal").ap()

        z_ps = [ctx.enter_context(nc.psum_tensor(f"z_ps{i}", [P, T], F32)) for i in range(NZ)]
        o_ps = [ctx.enter_context(nc.psum_tensor(f"o_ps{i}", [P, T], F32)) for i in range(NO)]
        xn_t = [o_ps[0], o_ps[1]]
        small_ps = z_ps[2]
        logits_ps = o_ps[2]
        combine_ps = o_ps[3]
        final_ps = [[o_ps[0], o_ps[1]], [z_ps[0], z_ps[1]]]

        x_loaded = [sem(f"x_loaded{b}") for b in range(B)]
        subject_loaded = sem("subject_loaded")
        params_loaded = sem("params_loaded")
        params2_loaded = sem("params2_loaded")
        y_init = sem("y_init")
        angles_loaded = sem("angles_loaded")
        w_first_loaded = sem("w_first_loaded")
        w_second_loaded = sem("w_second_loaded")
        w_rest_loaded = sem("w_rest_loaded")
        combine_stored = sem("combine_stored")
        cb_loaded = [sem(f"cb_loaded{q}") for q in range(GP)]
        cb_second_pair_loaded = sem("cb_second_pair_loaded")
        cb_rest_loaded = sem("cb_rest_loaded")
        out_stored = sem("out_stored")
        eps_ready = sem("eps_ready")
        consts_ready = sem("consts_ready")
        onehot_ready = sem("onehot_ready")
        subject_mm = sem("subject_mm")
        subject_act = sem("subject_act")
        soft_step = sem("soft_step")
        tok_mean_var = sem("tok_mean_var")
        g_ready = sem("g_ready")
        tok_seed = sem("tok_seed")
        tok_rstd = sem("tok_rstd")
        xn_by_dve = sem("xn_by_dve")
        xn_by_act = sem("xn_by_act")
        xn_t_ready = sem("xn_t_ready")
        t_mean_var = sem("t_mean_var")
        t_seed = sem("t_seed")
        affine_ready = sem("affine_ready")
        h_ready = sem("h_ready")
        h_hi_ready = sem("h_hi_ready")
        h_lo_ready = sem("h_lo_ready")
        logits_ready = sem("logits_ready")
        shifted_ready = sem("shifted_ready")
        e_prob_ready = sem("e_prob_ready")
        rank_ready = sem("rank_ready")
        combine_ready = sem("combine_ready")
        combine_t_ps = sem("combine_t_ps")
        combine_t_ready = sem("combine_t_ready")
        angles_ready = sem("angles_ready")
        sines_ready = sem("sines_ready")
        masks_ready = sem("masks_ready")
        pool_step = sem("pool_step")
        rot_ready = sem("rot_ready")
        dve_step = sem("dve_step")
        w_hi_ready = sem("w_hi_ready")
        w_hi_by_pool = sem("w_hi_by_pool")
        w_lo_ready = sem("w_lo_ready")
        z_ready = sem("z_ready")
        hid_ready = sem("hid_ready")
        hi_by_act = sem("hi_by_act")
        hi_by_dve = sem("hi_by_dve")
        lo_by_dve = sem("lo_by_dve")
        lo_by_pool = sem("lo_by_pool")
        unit_done = sem("unit_done")
        weighted_ready = sem("weighted_ready")
        y_added = sem("y_added")
        final_ready = sem("final_ready")
        out_ready = sem("out_ready")
        b1_copied = sem("b1_copied")

        block = ctx.enter_context(nc.Block())
        HALF = T // 2

        @block.sync
        def _(sp):
            def load_x(b):
                sp.dma_start(x_tok[:, b * TT:(b + 1) * TT, :], x_tokens[:, b]).then_inc(x_loaded[b], 16)

            def load_w(e, loaded):
                sp.dma_start(w_raw[:, e, :], exp_w[e]).then_inc(loaded, 16)

            load_x(0)
            sp.dma_start(ids[:, :], subject_ids.rearrange("(o b) -> o b", o=1).to_broadcast([S, B]))\
                .then_inc(subject_loaded, 16)
            sp.dma_start(packed[:, 0:PACK_FIRST], params[:, 0:PACK_FIRST]).then_inc(params_loaded, 16)
            load_x(1)
            sp.dma_start(packed[:, PACK_FIRST:], params[:, PACK_FIRST:]).then_inc(params2_loaded, 16)
            load_w(0, w_first_loaded)
            load_w(1, w_second_loaded)
            sp.dma_start(y_sum[:, :, :], x_features).then_inc(y_init, 16)
            for e in range(2, E):
                load_w(e, w_rest_loaded)
            sp.wait_ge(combine_t_ready, 1)
            sp.dma_start(combine_dram.rearrange("e (j p) -> (e j) p", p=P), combine_t[:, :])\
                .then_inc(combine_stored, 16)
            sp.wait_ge(combine_stored, 16)

            def load_combine(e, tokens, loaded):
                sp.dma_start(combine_all[:, e, tokens],
                             combine_dram[e:e + 1, tokens].to_broadcast([P, tokens.stop - tokens.start]))\
                    .then_inc(loaded, 16)

            load_combine(0, slice(0, T), cb_loaded[0])
            load_combine(1, slice(0, T), cb_loaded[1])
            load_combine(0, slice(T, B * T), cb_loaded[2])
            load_combine(1, slice(T, B * T), cb_loaded[3])
            for e in range(2, E):
                load_combine(e, slice(0, B * T), cb_second_pair_loaded if e < 4 else cb_rest_loaded)
            sp.wait_ge(out_ready, 2)
            sp.dma_start(out[:, 0], out_sb[:, 0]).then_inc(out_stored, 16)
            for half in range(2):
                cols = slice(half * HALF, (half + 1) * HALF)
                sp.wait_ge(out_ready, 3 + half)
                sp.dma_start(out[:, 1, cols], out_sb[:, 1, cols]).then_inc(out_stored, 16)
            sp.wait_ge(out_stored, 3 * 16)

        @block.gpsimd
        def _(pool):
            nc.gpsimd.iota(part[:, 0:1], [[0, 1]], base=0, channel_multiplier=1).then_inc(consts_ready, 1)
            nc.gpsimd.memset(ident[:, :], 0.0).then_inc(consts_ready, 1)
            pool.wait_ge(consts_ready, 2)
            nc.gpsimd.affine_select(out=ident[:, :], in_=ident[:, :], compare_op=ALU.not_equal, fill=1.0,
                                    base=0, pattern=[[-1, P]], channel_multiplier=1).then_inc(consts_ready, 1)
            nc.gpsimd.tensor_copy(part_f[:, 0:1], part[:, 0:1]).then_inc(consts_ready, 1)
            nc.gpsimd.tensor_scalar(part_f[:, 4:5], part[:, 0:1], -float(S), None, ALU.add).then_inc(consts_ready, 1)
            nc.gpsimd.memset(eps[:, 0:1], LN_EPS).then_inc(eps_ready, 1)
            nc.gpsimd.memset(eps[:, 1:2], TIME_EPS).then_inc(eps_ready, 1)
            pool.wait_ge(subject_loaded, 16)
            pool.wait_ge(consts_ready, 5)
            nc.gpsimd.tensor_scalar(onehot[:, 0, :], ids[:, :], float(S - 1), part_f[0:S, 0:1],
                                    ALU.min, ALU.is_equal).then_inc(onehot_ready, 1)
            nc.gpsimd.tensor_scalar(onehot[:, 1, :], ids[:, :], -float(S), part_f[0:S, 4:5],
                                    ALU.max, ALU.is_equal).then_inc(onehot_ready, 1)
            for n, a in enumerate((theta, phi)):
                pool.dma_start(angles[:, n, :], a.rearrange("(o b) -> o b", o=1).to_broadcast([P, B]))\
                    .then_inc(angles_loaded, 16)
            nc.gpsimd.iota(rank_i[:, :, :], [[0, B * TT], [-1, E]], base=E, channel_multiplier=0)\
                .then_inc(consts_ready, 1)
            pool.wait_ge(consts_ready, 6)
            nc.gpsimd.tensor_copy(rank[:, :, :], rank_i[:, :, :]).then_inc(rank_ready, 1)
            for m in (above, below):
                nc.gpsimd.memset(m[:, :], 0.0).then_inc(consts_ready, 1)
            for n, (m, base) in enumerate(((above, 1), (below, -1))):
                pool.wait_ge(consts_ready, 7 + n)
                nc.gpsimd.affine_select(out=m[:, :], in_=m[:, :], compare_op=ALU.not_equal, fill=1.0,
                                        base=base, pattern=[[-1, P]], channel_multiplier=1)\
                    .then_inc(consts_ready, 1)

            def split_low(i, k, half, first=False, by_pool=False):
                cols = slice(half * FF, (half + 1) * FF)
                if by_pool:
                    pool.wait_ge(w_hi_by_pool, half + 1)
                elif first:
                    pool.wait_ge(w_hi_ready, half + 1)
                else:
                    pool.wait_ge(w_hi_ready, 4 * i + 2 * k + half - 1)
                nc.gpsimd.tensor_tensor(w_lo[k % 2][:, cols], w_raw[:, 2 * i + k, cols],
                                        w_hi[k % 2][:, cols].bitcast(F32), ALU.subtract)\
                    .then_inc(w_lo_ready, 1)

            done = [0]

            def settle(ins):
                done[0] += 1
                ins.then_inc(pool_step, 1)
                pool.wait_ge(pool_step, done[0])

            def sine_arguments():
                tt, ts = nc.gpsimd.tensor_tensor, nc.gpsimd.tensor_scalar
                pool.wait_ge(angles_loaded, 32)
                pool.wait_ge(masks_ready, 2)
                settle(ts(ang[:, 0, :], angles[:, 0, :], part_f[:, 2:3], None, ALU.mult))
                settle(ts(ang[:, 1, :], angles[:, 1, :], part_f[:, 1:2], None, ALU.mult))
                settle(tt(ang[:, 2, :], ang[:, 0, :], ang[:, 1, :], ALU.add))
                settle(ts(ang[:, 3, :], ang[:, 2, :], 1 / (2 * math.pi), ROUND, ALU.mult, ALU.add))
                settle(ts(ang[:, 4, :], ang[:, 3, :], -ROUND, None, ALU.add))
                settle(ts(ang[:, 5, :], ang[:, 4, :], -TWO_PI_HIGH, None, ALU.mult))
                settle(tt(ang[:, 6, :], ang[:, 2, :], ang[:, 5, :], ALU.add))
                settle(ts(ang[:, 5, :], ang[:, 4, :], -TWO_PI_LOW, None, ALU.mult))
                settle(tt(ang[:, 7, :], ang[:, 6, :], ang[:, 5, :], ALU.add))
                settle(ts(ang[:, 8, :], ang[:, 7, :], PI_BELOW, -PI_BELOW, ALU.min, ALU.max))
                settle(ts(ang[:, 7, :], ang[:, 8, :], 0.0, 2.0, ALU.max, ALU.mult))
                settle(tt(ang[:, 6, :], ang[:, 7, :], ang[:, 8, :], ALU.subtract))
                ts(ang[:, 9, :], ang[:, 6, :], -1.0, math.pi / 2, ALU.mult, ALU.add).then_inc(angles_ready, 1)

            def rotation(b):
                tt, ts = nc.gpsimd.tensor_tensor, nc.gpsimd.tensor_scalar
                pool.wait_ge(sines_ready, 2)
                settle(ts(ang[:, 0, :], ang[:, 10, :], part_f[:, 3:4], None, ALU.mult))
                settle(tt(ang[:, 1, :], ang[:, 0, :], ang[:, 10, :], ALU.subtract))
                for n, (m, c) in enumerate(((ident, 11), (below, 0), (above, 1))):
                    settle(ts(rot_t[:, n, :], m[:, :], ang[:, c, b:b + 1], None, ALU.mult))
                settle(tt(rot_t[:, 0, :], rot_t[:, 0, :], rot_t[:, 1, :], ALU.add))
                tt(rot[:, b, :], rot_t[:, 0, :], rot_t[:, 2, :], ALU.add).then_inc(rot_ready, 1)
                pool.wait_ge(rot_ready, b + 1)

            def add_group(i, q, first=False):
                pool.wait_ge(weighted_ready, GP * i + q + 1)
                b = q // 2 if first else q % B
                if first and q % 2 == 0:
                    pool.wait_ge(y_init, 16)
                elif first:
                    pool.wait_ge(y_added, q)
                else:
                    pool.wait_ge(y_added, GP * i + q - B + 1)
                nc.gpsimd.tensor_tensor(y_sum[:, b, :], y_sum[:, b, :], weighted[q % NT][:, :], ALU.add)\
                    .then_inc(y_added, 1)

            def copy_high(half):
                cols = slice(half * FF, (half + 1) * FF)
                nc.gpsimd.tensor_copy(w_hi[1][:, cols], w_raw[:, 1, cols]).then_inc(w_hi_by_pool, 1)

            split_low(0, 0, 0, first=True)
            pool.wait_ge(w_second_loaded, 16)
            copy_high(0)
            split_low(0, 0, 1, first=True)
            split_low(0, 1, 0, by_pool=True)
            copy_high(1)
            split_low(0, 1, 1, by_pool=True)
            for k in POOL_LOWS:
                pool.wait_ge(hid_ready, k + 1)
                if k >= NZ:
                    pool.wait_ge(unit_done, k - NZ + 1)
                nc.gpsimd.tensor_tensor(hid_lo[k % NZ][:, :], hid[k % NR][:, :],
                                        hid_hi[k % NZ][:, :].bitcast(F32), ALU.subtract).then_inc(lo_by_pool, 1)
            split_low(0, 2, 0)
            sine_arguments()
            split_low(0, 2, 1)
            for q in range(GP - 1):
                add_group(0, q, first=True)
            pool.wait_ge(y_added, GP - 1)
            with pool.Fori(1, PAIRS - 1) as i:
                split_low(i, 1, 0)
                add_group(i, -1)
                split_low(i, 1, 1)
                add_group(i, 0)
                add_group(i, 1)
                split_low(i, 2, 0)
                split_low(i, 2, 1)
                add_group(i, 2)
            rotation(0)
            split_low(PAIRS - 1, 1, 0)
            add_group(PAIRS - 1, -1)
            split_low(PAIRS - 1, 1, 1)
            rotation(1)
            for q in range(GP - 1):
                add_group(PAIRS - 1, q)

        @block.scalar
        def _(act):
            nc.scalar.preload_act_table_set("natural_log_exp_and_others")

            def seed(b):
                act.wait_ge(tok_mean_var, TT * (b + 1))
                nc.scalar.activation(tok_s[:, b, LN, :], mean_var[:, b * TT:(b + 1) * TT, 1], ACT.Ln,
                                     bias=eps[:, 0:1]).then_inc(tok_seed, 1)
                act.wait_ge(tok_seed, 2 * b + 1)
                nc.scalar.activation(tok_s[:, b, SEED, :], tok_s[:, b, LN, :], ACT.Exp, scale=-0.5)\
                    .then_inc(tok_seed, 1)

            def normalise_rest(b):
                act.wait_ge(tok_rstd, 2 * (b + 1))
                for t in range(DT, TT):
                    nc.scalar.activation(xn_tok[:, b * TT + t, :], x_tok[:, b * TT + t, :], ACT.Identity,
                                         scale=tok_s[:, b, RSTD, t:t + 1], bias=tok_s[:, b, SHIFT, t:t + 1])\
                        .then_inc(xn_by_act, 1)

            def time_ln(b):
                act.wait_ge(t_mean_var, b + 1)
                nc.scalar.activation(t_s[:, b, LN:LN + 1], t_mv[:, b, 1:2], ACT.Ln, scale=g_squared[:, 0:1],
                                     bias=eps[:, 1:2]).then_inc(t_seed, 1)

            def time_exp(b):
                act.wait_ge(t_seed, 2 * b + 1)
                nc.scalar.activation(t_s[:, b, SEED:SEED + 1], t_s[:, b, LN:LN + 1], ACT.Exp, scale=-0.5)\
                    .then_inc(t_seed, 1)

            def h_high(b):
                act.wait_ge(affine_ready, 2 * (b + 1))
                nc.scalar.activation(h_hi[:, b, :], xn_t[b][:, :], ACT.Identity,
                                     scale=t_s[:, b, SCALE:SCALE + 1], bias=t_s[:, b, BIAS:BIAS + 1])\
                    .then_inc(h_hi_ready, 1)

            def h_float(b):
                act.wait_ge(affine_ready, 2 * (b + 1))
                nc.scalar.activation(h_all[:, b, :], xn_t[b][:, :], ACT.Identity,
                                     scale=t_s[:, b, SCALE:SCALE + 1], bias=t_s[:, b, BIAS:BIAS + 1])\
                    .then_inc(h_ready, 1)

            def split_high(i, k, half):
                cols = slice(half * FF, (half + 1) * FF)
                nc.scalar.activation(w_hi[k % 2][:, cols], w_raw[:, 2 * i + k, cols], ACT.Copy)\
                    .then_inc(w_hi_ready, 1)

            act.wait_ge(eps_ready, 2)
            act.wait_ge(subject_mm, 1)
            nc.scalar.copy(emb_t[:, :], small_ps[0:SE, 0:B]).then_inc(subject_act, 1)
            seed(0)
            act.wait_ge(subject_mm, 2)
            nc.scalar.activation(hyp_1[:, :], small_ps[:, 2:2 + B], ACT.Relu, bias=param("hyp_b1"))\
                .then_inc(subject_act, 1)
            act.wait_ge(subject_mm, 3)
            nc.scalar.activation(hyp_2[:, :], small_ps[:, 4:4 + B], ACT.Identity, bias=param("hyp_b2"))\
                .then_inc(subject_act, 1)
            normalise_rest(0)
            act.wait_ge(subject_mm, 4)
            nc.scalar.activation(sty_1[:, :], small_ps[0:SH // 2, 6:6 + B], ACT.Relu, bias=param("sty_b1"))\
                .then_inc(subject_act, 1)
            seed(1)
            act.wait_ge(w_first_loaded, 16)
            split_high(0, 0, 0)
            act.wait_ge(subject_mm, 5)
            graw, braw = small_ps[:, 8:8 + B], small_ps[:, 10:10 + B]
            gamma_b, beta_b = param("sty_b2")[:, 0:1], param("sty_b2")[:, 1:2]
            nc.scalar.activation(soft[:, 0:B], graw, ACT.Abs, bias=gamma_b).then_inc(soft_step, 1)
            nc.scalar.activation(soft[:, 3 * B:4 * B], graw, ACT.Relu, bias=gamma_b).then_inc(soft_step, 1)
            act.wait_ge(soft_step, 1)
            nc.scalar.activation(soft[:, B:2 * B], soft[:, 0:B], ACT.Exp, scale=-1.0).then_inc(soft_step, 1)
            act.wait_ge(g_ready, 1)
            time_ln(0)
            act.wait_ge(soft_step, 3)
            nc.scalar.activation(soft[:, 2 * B:3 * B], soft[:, B:2 * B], ACT.Ln, bias=1.0).then_inc(soft_step, 1)
            time_exp(0)
            nc.scalar.activation(beta[:, :], braw, ACT.Identity, bias=beta_b).then_inc(soft_step, 1)

            def copy_b1(i, k):
                nc.scalar.copy(b1_now[k % 2][:, :], b1_cols[:, bass.ds((2 * i + k) * FC, FC)])\
                    .then_inc(b1_copied, 1)

            def hidden(i, k, first):
                u = UP * i + k
                parity, _, c = unit_parts(k, first)
                bias = b1_now[parity][:, c:c + 1]
                act.wait_ge(z_ready, u + 1)
                if k % 2 == 0 or first and k in ACT_HIGHS:
                    if not (first and k < NZ):
                        act.wait_ge(unit_done, u - NZ + 1)
                    nc.scalar.activation(hid_hi[k % NZ][:, :], z_ps[k % NZ][:, :], ACT.Relu, bias=bias)\
                        .then_inc(hi_by_act, 1)
                if first and k - NR in POOL_LOWS:
                    act.wait_ge(lo_by_pool, POOL_LOWS.index(k - NR) + 1)
                elif not first or k >= NR:
                    act.wait_ge(lo_by_dve, lows_by_dve(i, k - NR, first))
                nc.scalar.activation(hid[k % NR][:, :], z_ps[k % NZ][:, :], ACT.Relu, bias=bias)\
                    .then_inc(hid_ready, 1)

            split_high(0, 0, 1)
            h_high(0)
            h_float(0)
            normalise_rest(1)
            copy_b1(0, 0)
            copy_b1(0, 1)

            def exponentials():
                act.wait_ge(shifted_ready, 1)
                nc.scalar.activation(e_prob[:, :, :], shifted[:, :, :], ACT.Exp).then_inc(e_prob_ready, 1)

            def combine_columns():
                act.wait_ge(combine_t_ps, 1)
                nc.scalar.copy(combine_t[:, :], combine_ps[0:E * B * TT, 0:P]).then_inc(combine_t_ready, 1)

            def sines():
                act.wait_ge(angles_ready, 1)
                nc.scalar.activation(ang[:, 10, :], ang[:, 8, :], ACT.Sin).then_inc(sines_ready, 1)
                nc.scalar.activation(ang[:, 11, :], ang[:, 9, :], ACT.Sin).then_inc(sines_ready, 1)

            def pair(i, last=False):
                for k in range(UP):
                    if k % UE == 0:
                        act.wait_ge(b1_copied, 2 * i + k // UE + 1)
                    hidden(i, k, first=False)
                    if last and k == SINES_AT:
                        sines()
                    half = k % UE - SPLIT_AT
                    if half in (0, 1) and not (last and k >= UE):
                        if half == 0:
                            copy_b1(i, k // UE + 1)
                        split_high(i, k // UE + 1, half)

            for k in range(UP):
                if k in (0, FC):
                    act.wait_ge(b1_copied, k // FC + 1)
                hidden(0, k, first=True)
                if k == 1:
                    time_ln(1)
                    time_exp(1)
                elif k == 3:
                    h_float(1)
                elif k == 4:
                    h_high(1)
                elif k == EXP_AT:
                    exponentials()
                elif k == COMBINE_T_AT:
                    combine_columns()
                if k == UP - FC:
                    act.wait_ge(w_rest_loaded, (E - 2) * 16)
                    act.wait_ge(hid_ready, UP - FC)
                    copy_b1(0, 2)
                    split_high(0, 2, 0)
                elif k == UP - 1:
                    act.wait_ge(unit_done, UP - FC)
                    split_high(0, 2, 1)
            with act.Fori(1, PAIRS - 1) as i:
                pair(i)
            pair(PAIRS - 1, last=True)
            for b in range(B):
                for half in range(2):
                    act.wait_ge(final_ready, 2 * b + half + 1)
                    nc.scalar.copy(out_sb[:, b, half * HALF:(half + 1) * HALF], final_ps[b][half][:, 0:HALF])\
                        .then_inc(out_ready, 1)

        @block.vector
        def _(dve):
            done = [0]

            def step(ins):
                done[0] += 1
                ins.then_inc(dve_step, 1)
                return done[0]

            def settle(ins):
                dve.wait_ge(dve_step, step(ins))

            def token_stats(b, tiles):
                dve.wait_ge(x_loaded[b], 16)
                for t in tiles:
                    n = step(nc.vector.bn_stats(stats[:, b * TT + t, :], x_tok[:, b * TT + t, :]))
                return n - len(tiles)

            def token_variances(b, n):
                s = tok_s[:, b]
                for t in range(TT):
                    dve.wait_ge(dve_step, n + 1 + t)
                    nc.vector.bn_aggr(mean_var[:, b * TT + t, :], stats[:, b * TT + t, :]).then_inc(tok_mean_var, 1)
                dve.wait_ge(tok_mean_var, TT * (b + 1))
                step(nc.vector.tensor_scalar(s[:, HALF_VAR, :], mean_var[:, b * TT:(b + 1) * TT, 1], -0.5,
                                             -LN_EPS / 2, ALU.mult, ALU.add))

            def token_rstd(b):
                s = tok_s[:, b]
                dve.wait_ge(tok_seed, 2 * (b + 1))
                settle(nc.vector.tensor_tensor(s[:, SQUARE, :], s[:, SEED, :], s[:, SEED, :], ALU.mult))
                settle(nc.vector.tensor_tensor(s[:, SQUARE_VAR, :], s[:, SQUARE, :], s[:, HALF_VAR, :], ALU.mult))
                nc.vector.scalar_tensor_tensor(s[:, RSTD, :], s[:, SQUARE_VAR, :], 1.5, s[:, SEED, :],
                                               ALU.add, ALU.mult).then_inc(tok_rstd, 1)
                dve.wait_ge(tok_rstd, 2 * b + 1)
                nc.vector.scalar_tensor_tensor(s[:, SHIFT, :], mean_var[:, b * TT:(b + 1) * TT, 0], -1.0,
                                               s[:, RSTD, :], ALU.mult, ALU.mult).then_inc(tok_rstd, 1)

            def normalise(b):
                for t in range(DT):
                    nc.vector.tensor_scalar(xn_tok[:, b * TT + t, :], x_tok[:, b * TT + t, :],
                                            mean_var[:, b * TT + t, 0:1], tok_s[:, b, RSTD, t:t + 1],
                                            ALU.subtract, ALU.mult).then_inc(xn_by_dve, 1)

            def time_stats(b):
                s = t_s[:, b]
                dve.wait_ge(xn_t_ready, b + 1)
                settle(nc.vector.bn_stats(t_stats[:, b, :], xn_t[b][:, :]))
                nc.vector.bn_aggr(t_mv[:, b, :], t_stats[:, b, :]).then_inc(t_mean_var, 1)
                dve.wait_ge(t_mean_var, b + 1)
                step(nc.vector.tensor_scalar(s[:, HALF_VAR:HALF_VAR + 1], t_mv[:, b, 1:2], g_squared[:, 1:2],
                                             -TIME_EPS / 2, ALU.mult, ALU.add))
                settle(nc.vector.tensor_scalar(s[:, SQUARE:SQUARE + 1], t_mv[:, b, 0:1], ln_g, ln_b,
                                               ALU.mult, ALU.add))
                settle(nc.vector.tensor_scalar(s[:, MEAN:MEAN + 1], s[:, SQUARE:SQUARE + 1], ln_b, -1.0,
                                               ALU.subtract, ALU.mult))

            def affine(b):
                s = t_s[:, b]

                def col(n):
                    return s[:, n:n + 1]
                dve.wait_ge(t_seed, 2 * (b + 1))
                n = step(nc.vector.tensor_scalar(col(SQUARE_VAR), col(SEED), col(SEED), col(HALF_VAR),
                                                 ALU.mult, ALU.mult))
                dve.wait_ge(dve_step, n - 1)
                step(nc.vector.tensor_scalar(col(WIDTH), gamma[:, b:b + 1], ln_g, None, ALU.mult))
                dve.wait_ge(dve_step, n)
                n = step(nc.vector.tensor_scalar(col(RSTD), col(SQUARE_VAR), 1.5, col(SEED), ALU.add, ALU.mult))
                step(nc.vector.tensor_scalar(col(OFFSET), gamma[:, b:b + 1], col(MEAN), None, ALU.mult))
                dve.wait_ge(dve_step, n)
                nc.vector.tensor_scalar(col(SCALE), col(RSTD), col(WIDTH), None, ALU.mult).then_inc(affine_ready, 1)
                dve.wait_ge(dve_step, n + 1)
                dve.wait_ge(soft_step, 5)
                nc.vector.tensor_scalar(col(BIAS), col(RSTD), col(OFFSET), beta[:, b:b + 1], ALU.mult, ALU.add)\
                    .then_inc(affine_ready, 1)

            def feature_masks():
                dve.wait_ge(consts_ready, 4)
                step(nc.vector.tensor_scalar(part[:, 1:2], part[:, 0:1], 2, None, ALU.bitwise_and))
                n = step(nc.vector.tensor_scalar(part_odd[:, :], part[:, 0:1], 1, None, ALU.bitwise_and))
                dve.wait_ge(dve_step, n)
                n = step(nc.vector.tensor_scalar(part_f[:, 1:2], part[:, 1:2], 0.5, None, ALU.mult))
                nc.vector.tensor_copy(part_f[:, 3:4], part_odd[:, :]).then_inc(masks_ready, 1)
                dve.wait_ge(dve_step, n)
                nc.vector.tensor_scalar(part_f[:, 2:3], part_f[:, 1:2], -1.0, 1.0, ALU.mult, ALU.add)\
                    .then_inc(masks_ready, 1)

            def split_h(b):
                dve.wait_ge(h_ready, b + 1)
                dve.wait_ge(h_hi_ready, b + 1)
                nc.vector.tensor_tensor(h_lo[:, b, :], h_all[:, b, :], h_hi[:, b, :].bitcast(F32), ALU.subtract)\
                    .then_inc(h_lo_ready, 1)

            n = token_stats(0, range(TT))
            token_variances(0, n)
            token_stats(1, range(2))
            token_rstd(0)
            normalise(0)
            n = token_stats(1, range(2, TT))
            token_variances(1, n - 2)
            dve.wait_ge(params_loaded, 16)
            settle(nc.vector.tensor_tensor(g_squared[:, 0:1], ln_g, ln_g, ALU.mult))
            nc.vector.tensor_scalar(g_squared[:, 1:2], g_squared[:, 0:1], -0.5, None, ALU.mult).then_inc(g_ready, 1)
            dve.wait_ge(g_ready, 1)
            time_stats(0)
            dve.wait_ge(soft_step, 4)
            step(nc.vector.scalar_tensor_tensor(gamma[:, :], soft[:, 2 * B:3 * B], GAMMA_EPS,
                                                soft[:, 3 * B:4 * B], ALU.add, ALU.add))
            affine(0)
            token_rstd(1)
            normalise(1)
            split_h(0)
            time_stats(1)

            def over(m):
                return red[:, m, :].unsqueeze(2).to_broadcast([P, B * TT, E])

            def reduce(m, src, op):
                settle(nc.vector.tensor_reduce(red[:, m, :], src[:, :, :], axis=AX_X, op=op))

            def tt(o, a, b_, op):
                settle(nc.vector.tensor_tensor(o[:, :, :], a[:, :, :], b_, op))

            def largest(m, src):
                reduce(m, src, ALU.max)
                tt(pick, src, over(m), ALU.is_equal)
                tt(pick, pick, rank[:, :, :], ALU.mult)

            def first_of(m, mask):
                reduce(m, pick, ALU.max)
                tt(mask, rank, over(m), ALU.is_equal)

            def shift_logits():
                dve.wait_ge(logits_ready, B)
                logits = logits_ps[:, 0:B * TT * E].rearrange("p (j e) -> p j e", e=E)
                settle(nc.vector.tensor_reduce(red[:, 0, :], logits, axis=AX_X, op=ALU.max))
                nc.vector.tensor_tensor(shifted[:, :, :], logits, over(0), ALU.subtract).then_inc(shifted_ready, 1)

            def probabilities():
                dve.wait_ge(e_prob_ready, 1)
                reduce(1, e_prob, ALU.add)
                settle(nc.vector.reciprocal(red[:, 2, :], red[:, 1, :]))
                tt(prob, e_prob, over(2), ALU.mult)

            def first_choice_ranks():
                dve.wait_ge(rank_ready, 1)
                largest(3, prob)

            def first_choice():
                first_of(4, mask1)
                settle(nc.vector.scalar_tensor_tensor(rest[:, :, :], mask1[:, :, :], -2.0, prob[:, :, :],
                                                      ALU.mult, ALU.add))

            def second_choice_ranks():
                largest(5, rest)

            def combine_weights():
                first_of(6, mask2)
                tt(mask1, mask1, mask2[:, :, :], ALU.add)
                tt(gates, prob, mask1[:, :, :], ALU.mult)
                reduce(7, gates, ALU.add)
                settle(nc.vector.reciprocal(red[:, 8, :], red[:, 7, :]))
                nc.vector.tensor_tensor(combine[:, :, :].rearrange("p e j -> p j e"), gates[:, :, :], over(8),
                                        ALU.mult).then_inc(combine_ready, 1)

            def split_unit(i, k, first):
                dve.wait_ge(hid_ready, UP * i + k + 1)
                if not (first and k < NZ):
                    dve.wait_ge(unit_done, UP * i + k - NZ + 1)
                if k % 2 == 1 and not (first and k in ACT_HIGHS):
                    nc.vector.tensor_copy(hid_hi[k % NZ][:, :], hid[k % NR][:, :]).then_inc(hi_by_dve, 1)
                    dve.wait_ge(hi_by_dve, highs_by_dve(i, k, first))
                nc.vector.tensor_tensor(hid_lo[k % NZ][:, :], hid[k % NR][:, :],
                                        hid_hi[k % NZ][:, :].bitcast(F32), ALU.subtract).then_inc(lo_by_dve, 1)

            def weigh_group(i, q, first=False):
                b, e = (q // 2, q % 2) if first else (q % B, 2 * i + q // B)
                dve.wait_ge(unit_done, UP * i + (q + 1) * FC)
                if not (first and q < NT):
                    dve.wait_ge(y_added, GP * i + q - NT + 1)
                nc.vector.scalar_tensor_tensor(weighted[q % NT][:, :], o_ps[q % NO][:, :],
                                               b2_cols[:, bass.ds(e, 1)],
                                               combine_all[:, e, b * T:(b + 1) * T], ALU.add, ALU.mult)\
                    .then_inc(weighted_ready, 1)

            for k in range(UP + DVE_FROM):
                if k not in POOL_LOWS:
                    split_unit(0, k, first=True)
                if k == 1:
                    affine(1)
                if k == ROUTE_AT:
                    shift_logits()
                    split_h(1)
                elif k == ROUTE_AT + 1:
                    probabilities()
                elif k == ROUTE_AT + 2:
                    first_choice_ranks()
                elif k == ROUTE_AT + 3:
                    first_choice()
                elif k == ROUTE_AT + 4:
                    second_choice_ranks()
                elif k == ROUTE_AT + 5:
                    combine_weights()
                if k == UP - FC:
                    feature_masks()
                if k in FIRST_WEIGHED:
                    dve.wait_ge(cb_loaded[FIRST_WEIGHED[k]], 16)
                    weigh_group(0, FIRST_WEIGHED[k], first=True)
            dve.wait_ge(cb_second_pair_loaded, 2 * 16)
            with dve.Fori(1, PAIRS - 1) as i:
                for k in range(DVE_FROM, UP + DVE_FROM):
                    split_unit(i, k, first=False)
                    if k % FC == WEIGH_AT:
                        weigh_group(i, k // FC - 1)
                    if k == UP:
                        dve.wait_ge(cb_rest_loaded, (E - 4) * 16)
            for k in range(DVE_FROM, UP):
                split_unit(PAIRS - 1, k, first=False)
                if k % FC == WEIGH_AT:
                    weigh_group(PAIRS - 1, k // FC - 1)
            dve.wait_ge(unit_done, E * UE)
            last_weights = combine_all[:, E - 1, (B - 1) * T:B * T]
            for half in range(2):
                cols = slice(half * HALF, (half + 1) * HALF)
                nc.vector.scalar_tensor_tensor(weighted[-1][:, cols], o_ps[-1][:, cols], b2_cols[:, E - 1:E],
                                               last_weights[:, cols], ALU.add, ALU.mult)\
                    .then_inc(weighted_ready, 1)

        @block.tensor
        def _(pe):
            def mm(o, l, r, start=True, stop=True):
                return nc.tensor.matmul(o, l, r, start=start, stop=stop)

            def transposed(o, i, n=P):
                return nc.tensor.transpose(o, i, ident[0:n, 0:n])

            def keep_warm(n, cols=P):
                for _ in range(n):
                    mm(z_ps[3][:, 0:cols], ident[:, :], ident[:, 0:cols])

            def transpose_tokens(b, tiles=range(TT)):
                for t in tiles:
                    if t < DT:
                        pe.wait_ge(xn_by_dve, b * DT + t + 1)
                    else:
                        pe.wait_ge(xn_by_act, b * (TT - DT) + t - DT + 1)
                    m = transposed(xn_t[b][:, t * P:(t + 1) * P], xn_tok[:, b * TT + t, :])
                if t == TT - 1:
                    m.then_inc(xn_t_ready, 1)

            pe.wait_ge(consts_ready, 3)
            pe.wait_ge(params_loaded, 16)
            for n in range(2):
                pe.wait_ge(onehot_ready, n + 1)
                m = mm(small_ps[0:SE, 0:B], param("subj_emb"), onehot[:, n, :], n == 0, n == 1)
            m.then_inc(subject_mm, 1)
            pe.wait_ge(subject_act, 1)
            mm(small_ps[:, 2:2 + B], param("hyp_w1"), emb_t[:, :]).then_inc(subject_mm, 1)
            pe.wait_ge(params2_loaded, 16)
            pe.wait_ge(subject_act, 2)
            mm(small_ps[:, 4:4 + B], param("hyp_w2"), hyp_1[:, :]).then_inc(subject_mm, 1)
            transpose_tokens(0, [0])
            pe.wait_ge(subject_act, 3)
            mm(small_ps[0:SH // 2, 6:6 + B], param("sty_w1"), hyp_2[:, :]).then_inc(subject_mm, 1)
            transpose_tokens(0, range(1, TT))
            pe.wait_ge(subject_act, 4)
            mm(small_ps[:, 8:8 + B], param("sty_w2")[:, 0:P], sty_1[:, :])
            mm(small_ps[:, 10:10 + B], param("sty_w2")[:, P:2 * P], sty_1[:, :]).then_inc(subject_mm, 1)

            def high_passes(i, k, first=False):
                parity, b, c = unit_parts(k, first)
                if k in ((0, FC) if first else (0, UE)):
                    pe.wait_ge(w_lo_ready, 4 * i + 2 * parity + 1)
                if not (first and k < NZ):
                    pe.wait_ge(hid_ready, UP * i + k - NZ + 1)
                elif k == 2:
                    pe.wait_ge(soft_step, 5)
                if first and k in (0, UE):
                    pe.wait_ge(h_hi_ready, b + 1)
                z = z_ps[k % NZ][:, :]
                cols = slice(c * P, (c + 1) * P)
                mm(z, w_hi[parity][:, cols], h_hi[:, b, :], True, False)
                mm(z, w_lo[parity][:, cols], h_hi[:, b, :], False, False)

            def low_pass(k, first=False):
                parity, b, c = unit_parts(k, first)
                if first and k in (0, UE):
                    pe.wait_ge(h_lo_ready, b + 1)
                mm(z_ps[k % NZ][:, :], w_hi[parity][:, c * P:(c + 1) * P], h_lo[:, b, :], False, True)\
                    .then_inc(z_ready, 1)

            def second_product(i, k, first=False):
                parity, _, c = unit_parts(k % UP, first)
                if k in ((0, FC) if first else (0, UE)):
                    pe.wait_ge(w_lo_ready, 4 * i + 2 * parity + 2)
                if c == 0:
                    if not first:
                        pe.wait_ge(weighted_ready, GP * i + k // FC - NO + 1)
                    elif k < 2 * FC:
                        pe.wait_ge(h_ready, k // FC + 1)
                        pe.wait_ge(h_hi_ready, k // FC + 1)
                    elif k == 2 * FC:
                        pe.wait_ge(shifted_ready, 1)
                    elif k == 3 * FC:
                        pe.wait_ge(combine_t_ready, 1)
                o = o_ps[k // FC % NO][:, :]
                cols = slice(FF + c * P, FF + (c + 1) * P)
                if k % 2 == 0 or first and k in ACT_HIGHS:
                    pe.wait_ge(hi_by_act, highs_by_act(i, k, first))
                else:
                    pe.wait_ge(hi_by_dve, highs_by_dve(i, k, first))
                mm(o, w_hi[parity][:, cols], hid_hi[k % NZ][:, :], c == 0, False)
                mm(o, w_lo[parity][:, cols], hid_hi[k % NZ][:, :], False, False)
                if first and k in POOL_LOWS:
                    pe.wait_ge(lo_by_pool, POOL_LOWS.index(k) + 1)
                else:
                    pe.wait_ge(lo_by_dve, lows_by_dve(i, k, first))
                mm(o, w_hi[parity][:, cols], hid_lo[k % NZ][:, :], False, c == FC - 1).then_inc(unit_done, 1)

            def logits(b):
                pe.wait_ge(h_ready, b + 1)
                for j in range(b * TT, (b + 1) * TT):
                    m = mm(logits_ps[:, j * E:(j + 1) * E], h_all[:, b, (j % TT) * P:(j % TT + 1) * P],
                           param("router_w"))
                m.then_inc(logits_ready, 1)

            def combine_transpose():
                pe.wait_ge(combine_ready, 1)
                transposed(combine_ps[0:E * B * TT, 0:P], combine[:, :, :].rearrange("p e j -> p (e j)"))\
                    .then_inc(combine_t_ps, 1)

            keep_warm(WARM_UP)
            high_passes(0, 0, first=True)
            high_passes(0, 1, first=True)
            transpose_tokens(1)
            low_pass(0, first=True)
            low_pass(1, first=True)
            high_passes(0, 2, first=True)
            low_pass(2, first=True)
            for k in range(LEAD, UP):
                if k == LOGITS_AT:
                    logits(1)
                high_passes(0, k, first=True)
                low_pass(k, first=True)
                if k == LEAD:
                    logits(0)
                second_product(0, k - LEAD, first=True)
                if k == COMBINE_T_AT:
                    combine_transpose()
            with pe.Fori(1, PAIRS) as i:
                for k in range(UP):
                    high_passes(i, k)
                    low_pass(k)
                    second_product(i, k - LEAD)

            def final_sum(b, half, stop):
                cols = slice(half * HALF, (half + 1) * HALF)
                return mm(final_ps[b][half][:, 0:HALF], rot[:, b, :], y_sum[:, b, cols], True, stop)

            for k in range(-LEAD, -1):
                second_product(PAIRS, k)
            pe.wait_ge(hid_ready, E * UE - 2)
            pe.wait_ge(rot_ready, B)
            pe.wait_ge(y_added, GROUPS - 2)
            for half in range(2):
                final_sum(1, half, False)
            second_product(PAIRS, -1)
            pe.wait_ge(y_added, GROUPS - 1)
            for half in range(2):
                final_sum(0, half, True).then_inc(final_ready, 1)
            for half in range(2):
                pe.wait_ge(weighted_ready, GROUPS + half)
                mm(final_ps[1][half][:, 0:HALF], rot[:, 1, :], weighted[-1][:, half * HALF:(half + 1) * HALF],
                   False, True).then_inc(final_ready, 1)


def kernel(**inputs):
    import numpy as np
    import concourse.bacc as bacc
    from concourse.bass_utils import run_bass_kernel_spmd

    own = {k.removeprefix("L0_cond_"): np.asarray(v) for k, v in inputs.items()}
    columns = {
        "subj_emb": own["subj_emb"], "hyp_w1": own["hyp_w1"], "hyp_w2": own["hyp_w2"],
        "sty_w1": own["sty_w1"], "sty_w2": own["sty_w2"], "router_w": own["router_w"],
        "hyp_b1": own["hyp_b1"][:, None], "hyp_b2": own["hyp_b2"][:, None], "sty_b1": own["sty_b1"][:, None],
        "ln_g": own["ln_g"][:, None], "ln_b": own["ln_b"][:, None],
        "sty_b2": own["sty_b2"].reshape(2, P).T,
        "exp_b1": own["exp_b1"].reshape(E * FC, P).T,
        "exp_b2": own["exp_b2"].T,
    }
    params = np.zeros((P, PACK_COLS), own["ln_g"].dtype)
    for name, (rows, start, cols) in PACK.items():
        params[0:rows, start:start + cols] = columns[name]
    w2_rows = own["exp_w2"].reshape(E, FC, P, P).transpose(0, 2, 1, 3).reshape(E, P, FF)
    arrays = {
        "x_tokens": own["x"].reshape(B, TT, P, P).transpose(2, 0, 1, 3),
        "x_features": own["x"].transpose(2, 0, 1),
        "subject_ids": own["itok_B_6_14"],
        "theta": own["condB_theta"],
        "phi": own["condB_phi"],
        "params": params,
        "exp_w": np.concatenate([own["exp_w1"], w2_rows], axis=2),
    }
    arrays = {f"{k}_dram": np.ascontiguousarray(v) for k, v in arrays.items()}

    nc = bacc.Bacc("TRN2", target_bir_lowering=False, num_devices=1)
    args = [nc.dram_tensor(k, v.shape, mybir.dt.from_np(v.dtype), kind="ExternalInput").ap()
            for k, v in arrays.items()]
    out = nc.dram_tensor("out_dram", (P, B, T), F32, kind="ExternalOutput").ap()
    conditioned_experts_kernel(nc, *args, out)
    got = run_bass_kernel_spmd(nc, [arrays], core_ids=[0]).results[0]["out_dram"]
    return np.ascontiguousarray(got.transpose(1, 2, 0))
```
